# Optimizing a Trainium2 kernel written in Bass

```python
import numpy as np
import jax
import jax.numpy as jnp

def _softmax(x, axis=-1):
    return jax.nn.softmax(x, axis=axis)

def _gelu(x):
    return jax.nn.gelu(x, approximate=True)

def _silu(x):
    return jax.nn.silu(x)

def _sigmoid(x):
    return jax.nn.sigmoid(x)

def _layernorm(x, axis=-1, eps=1e-05):
    m = jnp.mean(x, axis=axis, keepdims=True)
    v = jnp.var(x, axis=axis, keepdims=True)
    return (x - m) / jnp.sqrt(v + eps)

def _scatter_add(tgt, idx, src, axis=0):
    return tgt.at[idx].add(src)

def _segment_sum(src, seg, n):
    return jax.ops.segment_sum(src, seg, n)
kernel_name = 'mk_macaron_d1_jaxref_r4_631313'

def setup_inputs(seed: int=0):
    np.random.seed(seed)
    _w = jnp.asarray

    def _L0_attn_setup():
        import jax, jax.numpy as jnp
        import numpy as np
        B, T, C, H = (2, 512, 256, 16)
        HS = C // H

        def _rope_cos_sin(t, hs):
            pos = jnp.arange(t, dtype=jnp.float32)[:, None]
            i = jnp.arange(1, hs // 2 + 1, dtype=jnp.float32)[None]
            theta = 1.0 / 10000.0 ** (2.0 * (i - 1.0) / hs)
            ang = pos * theta
            return (jnp.cos(ang), jnp.sin(ang))

        def _apply_rope(u, cos, sin):
            u2 = u.reshape(*u.shape[:-1], HS // 2, 2)
            x0, x1 = (u2[..., 0], u2[..., 1])
            c = cos[None, None]
            s = sin[None, None]
            r0 = x0 * c - x1 * s
            r1 = x0 * s + x1 * c
            return jnp.stack([r0, r1], axis=-1).reshape(u.shape)
        key = jax.random.key(seed)
        ks = jax.random.split(key, 5)
        return {'x': jax.random.normal(ks[0], (B, T, C), dtype=jnp.float32), 'W_qkv': jax.random.normal(ks[1], (C, 3 * C), dtype=jnp.float32) * 0.02, 'b_qkv': jax.random.normal(ks[2], (3 * C,), dtype=jnp.float32) * 0.02, 'W_proj': jax.random.normal(ks[3], (C, C), dtype=jnp.float32) * 0.02, 'b_proj': jax.random.normal(ks[4], (C,), dtype=jnp.float32) * 0.02}
    _L0_attn_in = _L0_attn_setup()

    def _L0_ffn_setup():
        import jax, jax.numpy as jnp
        import numpy as np
        DIM = 256

        def _reference_tuple_inner(x, W_r, W_k, W_v, mu_r, mu_k):
            B, T, C = x.shape
            x_prev = jnp.concatenate([jnp.zeros((B, 1, C), x.dtype), x[:, :-1, :]], axis=1)
            xr = mu_r * x + (1.0 - mu_r) * x_prev
            xk = mu_k * x + (1.0 - mu_k) * x_prev
            r = jax.nn.sigmoid(jnp.einsum('btc,dc->btd', xr, W_r))
            k = jnp.einsum('btc,dc->btd', xk, W_k)
            k_act = jnp.square(jax.nn.relu(k))
            out = r * jnp.einsum('btc,dc->btd', k_act, W_v)
            new_state = x[:, -1, :]
            return (out, new_state)
        key = jax.random.key(seed)
        ks = jax.random.split(key, 6)
        B, T, C = (8, 512, DIM)
        x = jax.random.normal(ks[0], (B, T, C), dtype=jnp.float32)
        s = 1.0 / np.sqrt(C)
        W_r = jax.random.uniform(ks[1], (C, C), jnp.float32, -s, s)
        W_k = jax.random.uniform(ks[2], (C, C), jnp.float32, -s, s)
        W_v = jax.random.uniform(ks[3], (C, C), jnp.float32, -s, s)
        mu_r = jax.random.uniform(ks[4], (C,), jnp.float32)
        mu_k = jax.random.uniform(ks[5], (C,), jnp.float32)
        return {'x': x, 'W_r': W_r, 'W_k': W_k, 'W_v': W_v, 'mu_r': mu_r, 'mu_k': mu_k}
    _L0_ffn_in = _L0_ffn_setup()
    _d = {'L0_attn_x': _L0_attn_in['x'], 'L0_attn_W_qkv': _L0_attn_in['W_qkv'], 'L0_attn_b_qkv': _L0_attn_in['b_qkv'], 'L0_attn_W_proj': _L0_attn_in['W_proj'], 'L0_attn_b_proj': _L0_attn_in['b_proj'], 'L0_ffn_W_r': _L0_ffn_in['W_r'], 'L0_ffn_W_k': _L0_ffn_in['W_k'], 'L0_ffn_W_v': _L0_ffn_in['W_v'], 'L0_ffn_mu_r': _L0_ffn_in['mu_r'], 'L0_ffn_mu_k': _L0_ffn_in['mu_k']}
    _x0 = _d['L0_attn_x']
    _d['L0_attn_x'] = jax.random.normal(jax.random.fold_in(jax.random.key(seed), 1), (16, 1024, 256), dtype=_x0.dtype)
    del _x0
    return _d

def reference(L0_attn_x, L0_attn_W_qkv, L0_attn_b_qkv, L0_attn_W_proj, L0_attn_b_proj, L0_ffn_W_r, L0_ffn_W_k, L0_ffn_W_v, L0_ffn_mu_r, L0_ffn_mu_k):

    def _L0_attn_ref(x, W_qkv, b_qkv, W_proj, b_proj):
        import jax, jax.numpy as jnp
        import numpy as np
        B, T, C, H = (2, 512, 256, 16)
        HS = C // H

        def _rope_cos_sin(t, hs):
            pos = jnp.arange(t, dtype=jnp.float32)[:, None]
            i = jnp.arange(1, hs // 2 + 1, dtype=jnp.float32)[None]
            theta = 1.0 / 10000.0 ** (2.0 * (i - 1.0) / hs)
            ang = pos * theta
            return (jnp.cos(ang), jnp.sin(ang))

        def _apply_rope(u, cos, sin):
            u2 = u.reshape(*u.shape[:-1], HS // 2, 2)
            x0, x1 = (u2[..., 0], u2[..., 1])
            c = cos[None, None]
            s = sin[None, None]
            r0 = x0 * c - x1 * s
            r1 = x0 * s + x1 * c
            return jnp.stack([r0, r1], axis=-1).reshape(u.shape)
        b, t, c = x.shape
        qkv = x @ W_qkv + b_qkv
        qkv = qkv.reshape(b, t, H, 3 * HS).transpose(0, 2, 1, 3)
        q, k, v = jnp.split(qkv, 3, axis=-1)
        cos, sin = _rope_cos_sin(t, HS)
        q = _apply_rope(q, cos, sin)
        k = _apply_rope(k, cos, sin)
        att = jnp.einsum('bhqd,bhkd->bhqk', q, k) / jnp.sqrt(jnp.float32(HS))
        causal = jnp.tril(jnp.ones((t, t), dtype=bool))[None, None]
        att = jnp.where(causal, att, jnp.float32(-1000000000.0))
        att = jax.nn.softmax(att, axis=-1)
        y = jnp.einsum('bhqk,bhkd->bhqd', att, v)
        y = y.transpose(0, 2, 1, 3).reshape(b, t, c)
        return y @ W_proj + b_proj

    def _L0_ffn_ref(x, W_r, W_k, W_v, mu_r, mu_k):
        import jax, jax.numpy as jnp
        import numpy as np
        DIM = 256

        def _reference_tuple_inner(x, W_r, W_k, W_v, mu_r, mu_k):
            B, T, C = x.shape
            x_prev = jnp.concatenate([jnp.zeros((B, 1, C), x.dtype), x[:, :-1, :]], axis=1)
            xr = mu_r * x + (1.0 - mu_r) * x_prev
            xk = mu_k * x + (1.0 - mu_k) * x_prev
            r = jax.nn.sigmoid(jnp.einsum('btc,dc->btd', xr, W_r))
            k = jnp.einsum('btc,dc->btd', xk, W_k)
            k_act = jnp.square(jax.nn.relu(k))
            out = r * jnp.einsum('btc,dc->btd', k_act, W_v)
            new_state = x[:, -1, :]
            return (out, new_state)
        return _reference_tuple_inner(x, W_r, W_k, W_v, mu_r, mu_k)[0]
    x = L0_attn_x
    x = x + 0.5 * _L0_ffn_ref(_layernorm(x, axis=-1), L0_ffn_W_r, L0_ffn_W_k, L0_ffn_W_v, L0_ffn_mu_r, L0_ffn_mu_k)
    x = x + _L0_attn_ref(_layernorm(x, axis=-1), L0_attn_W_qkv, L0_attn_b_qkv, L0_attn_W_proj, L0_attn_b_proj)
    x = x + 0.5 * _L0_ffn_ref(_layernorm(x, axis=-1), L0_ffn_W_r, L0_ffn_W_k, L0_ffn_W_v, L0_ffn_mu_r, L0_ffn_mu_k)
    return x

_drawn_inputs = setup_inputs


def setup_inputs(seed=0):
    import zlib

    import numpy as np

    out = dict(_drawn_inputs(seed))
    spreads = {}
    factors = {'L0_attn_W_qkv': 6.229,
     'L0_attn_b_qkv': 8.0,
     'L0_attn_W_proj': 5.011,
     'L0_attn_b_proj': 2.919,
     'L0_ffn_W_r': 3.173,
     'L0_ffn_mu_r': 6.379}
    for name, (base, spread) in spreads.items():
        noise = np.random.default_rng([zlib.crc32(name.encode()), seed]).standard_normal(out[name].shape)
        drawn = base * np.exp(spread * noise) if base else spread * noise
        out[name] = jnp.asarray(drawn.astype(out[name].dtype))
    for name, factor in factors.items():
        out[name] = (out[name] * factor).astype(out[name].dtype)
    return out
```

```python
from contextlib import ExitStack

import numpy as np

import concourse.bass as bass
import concourse.mybir as mybir

F32 = mybir.dt.float32
BF16 = mybir.dt.bfloat16
ALU = mybir.AluOpType
ACT = mybir.ActivationFunctionType

P = 128
B, T, C = 16, 1024, 256
H, HS = 16, 16
EPS = 1e-5
CC = C // P
TT = T // P
CH = 256
CT = CH // P
NCH = T // CH
G = 4
NG = H // G
QC = 512
NQC = T // QC
KQ = QC // P
TERMS_Q = (0, 0, 0, 1, 1, 2)
TERMS_K = (0, 1, 2, 0, 1, 0)
NT = len(TERMS_Q)
KR = NT * HS
NP = 3
VW = HS + 1
VPAD = 32 - VW
NEG = -1e30
SCALE = HS ** -0.5


class Event:
    def __init__(self, sem, value):
        self.sem, self.value = sem, value


class Counter:

    def __init__(self, sem):
        self.sem, self.value = sem, 0

    def bump(self, by):
        self.value += by
        return Event(self, self.value)

    def now(self):
        return Event(self, self.value)


class Queue:

    def __init__(self):
        self.ops, self.reached = [], {}

    def wait(self, *events):
        for e in events:
            if e is not None and self.reached.get(e.sem, 0) < e.value:
                self.reached[e.sem] = e.value
                self.ops.append(lambda eng, s=e.sem.sem, v=e.value: eng.wait_ge(s, v))

    def do(self, make, after=(), sig=None, by=1):
        self.wait(*after)
        if sig is None:
            self.ops.append(make)
            return None
        self.ops.append(lambda eng, s=sig.sem: make(eng).then_inc(s, by))
        return sig.bump(by)

    def play(self, eng):
        for op in self.ops:
            op(eng)


def macaron(nc, x, w_r, w_k, w_v, mu_r, mu_k, w_qk, b_qk, w_vv, b_v, w_p, b_p, rope_c, rope_s, out, nb=B):
    ctx = ExitStack()
    with ctx:
        def sb(name, shape, dt=F32):
            return ctx.enter_context(nc.sbuf_tensor(name, shape, dt))

        def counter(name):
            return Counter(ctx.enter_context(nc.semaphore(name)))

        XR = 3
        x_sb = sb("x_sb", [P, XR, TT, C])
        xt_sb = sb("xt_sb", [P, 2, CT, C])
        xn_sb = sb("xn_sb", [P, 2, CC, CH + 1])
        dif_sb = sb("dif_sb", [P, 2, CC, CH])
        xk_sb = sb("xk_sb", [P, 2, CC, CH])
        ka_sb = sb("ka_sb", [P, 2, CC, CH])
        st_sb = sb("st_sb", [P, 2, CT, 6])
        mv_sb = sb("mv_sb", [P, 2, CT, 2])
        rs_sb = sb("rs_sb", [P, 2, CT])
        mhalf_sb = sb("mhalf_sb", [P, CT])
        qb_sb = sb("qb_sb", [P, 2, 2, CH])
        sw_sb = sb("sw_sb", [P, 2, 2, CH])
        part_sb = sb("part_sb", [P, NP, 4, T], BF16)
        v_sb = sb("v_sb", [P, 2, TT, H * VW + VPAD])
        qr_sb = sb("qr_sb", [P, 2, G, T], BF16)
        kr_sb = sb("kr_sb", [P, 2, G, T], BF16)
        pt_sb = sb("pt_sb", [P, 2, G, QC])
        yt_sb = sb("yt_sb", [P, 2, QC])
        den_sb = sb("den_sb", [P, 2, QC])
        yn_sb = sb("yn_sb", [P, NG, T])
        mx_sb = sb("mx_sb", [P, 2, G * TT])
        mres_sb = sb("mres_sb", [P, 2, G * TT])
        mp_sb = sb("mp_sb", [P, 2, NP, G * TT], BF16)
        mt_sb = sb("mt_sb", [P, 2, P], BF16)
        junk_sb = sb("junk_sb", [P, T], BF16)
        wr_sb = sb("wr_sb", [P, CC, C])
        wk_sb = sb("wk_sb", [P, CC, C])
        wv_sb = sb("wv_sb", [P, CC, C])
        wqk_sb = sb("wqk_sb", [P, CC, 2 * C])
        wvv_sb = sb("wvv_sb", [P, CC, C])
        wp_sb = sb("wp_sb", [P, NG, C])
        mur_sb = sb("mur_sb", [P, CC])
        muk_sb = sb("muk_sb", [P, CC])
        bqk_sb = sb("bqk_sb", [P, 4])
        bv_sb = sb("bv_sb", [P, C])
        cos_sb = sb("cos_sb", [P, T])
        sin_sb = sb("sin_sb", [P, T])
        mask_sb = sb("mask_sb", [P, T], BF16)
        id_sb = sb("id_sb", [P, P])
        idb_sb = sb("idb_sb", [P, P], BF16)

        ps_s = ctx.enter_context(nc.psum_tensor("ps_s", [P, 2, QC], F32))
        ps_m = ctx.enter_context(nc.psum_tensor("ps_m", [P, 2, T], F32))
        ps_y = ctx.enter_context(nc.psum_tensor("ps_y", [P, QC], F32))
        ps_d = ctx.enter_context(nc.psum_tensor("ps_d", [P, QC], F32))

        consts = counter("consts")
        x_in = [[counter(f"x_in{r}_{c}") for c in range(NCH)] for r in range(XR)]
        x_out = [[counter(f"x_out{r}_{c}") for c in range(NCH)] for r in range(XR)]
        swapped = [counter("swapped_q"), counter("swapped_k")]
        rows_in = [counter("rows_in0"), counter("rows_in1")]
        mrows_in = [counter("mrows_in0"), counter("mrows_in1")]
        pe_score = counter("pe_score")
        pe_maxs = counter("pe_maxs")
        pe_pv = counter("pe_pv")
        pe_dense = counter("pe_dense")
        act_exp = counter("act_exp")
        act_dense = counter("act_dense")
        dve_max = counter("dve_max")
        dve_dense = counter("dve_dense")
        pool_mask = counter("pool_mask")
        pool_dense = counter("pool_dense")
        setup = counter("setup")
        setup_dve = counter("setup_dve")

        pe, act, dve, pool, sp = (Queue() for _ in range(5))

        def chunked(w):
            return w.rearrange("(c p) n -> p c n", p=P)

        ev_zero = pool.do(lambda e: e.memset(wp_sb[:, :, :], 0.0), sig=setup)
        const_loads = [
            (wr_sb[:, :, :], chunked(w_r)), (wk_sb[:, :, :], chunked(w_k)), (wv_sb[:, :, :], chunked(w_v)),
            (wqk_sb[:, :, :], chunked(w_qk)), (wvv_sb[:, :, :], chunked(w_vv)),
            (mur_sb[:, :], mu_r), (muk_sb[:, :], mu_k), (bqk_sb[:, :], b_qk),
            (bv_sb[:, :], b_v.broadcast_to([P, C])), (cos_sb[:, :], rope_c), (sin_sb[:, :], rope_s),
        ]

        def load_x(b, c):
            r = b % XR
            src = x[b].rearrange("(t p) c -> p t c", p=P)[:, c * CT:(c + 1) * CT, :]
            return sp.do(lambda e: e.dma_start(x_sb[:, r, c * CT:(c + 1) * CT, :], src),
                         after=[x_out[r][c].now()], sig=x_in[r][c], by=16)

        x_ready = {}
        for c in range(NCH):
            x_ready[0, c] = load_x(0, c)
        for dst, src in const_loads:
            sp.do(lambda e, d=dst, s=src: e.dma_start(d, s), sig=consts, by=16)
        sp.wait(ev_zero)
        for g in range(NG):
            for j in range(G):
                h = G * g + j
                sp.do(lambda e, g=g, j=j, h=h: e.dma_start(wp_sb[32 * j:32 * j + HS, g, :], w_p[h * HS:(h + 1) * HS, :]),
                      sig=consts, by=16)
        sp.do(lambda e: e.dma_start(wp_sb[HS:HS + 1, 0, :], b_p), sig=consts, by=16)
        ev_const = consts.now()
        for b in range(1, min(nb, XR)):
            for c in range(NCH):
                x_ready[b, c] = load_x(b, c)

        pool.do(lambda e: e.memset(id_sb[:, :], 0.0), sig=setup)
        pool.do(lambda e: e.memset(idb_sb[:, :], 0.0), sig=setup)
        ev_mz = pool.do(lambda e: e.memset(mask_sb[:, :], 0.0), sig=setup)
        pool.wait(ev_mz)
        for t in (id_sb, idb_sb):
            pool.do(lambda e, t=t: e.affine_select(out=t[:, :], in_=t[:, :], compare_op=ALU.not_equal, fill=1.0,
                                                   base=0, pattern=[[-1, P]], channel_multiplier=1), sig=setup)
        pool.do(lambda e: e.affine_select(out=mask_sb[:, T - P:T], in_=mask_sb[:, T - P:T], compare_op=ALU.is_ge,
                                          fill=NEG, base=0, pattern=[[-1, P]], channel_multiplier=1), sig=setup)
        ev_ones = dve.do(lambda e: e.memset(kr_sb[KR:KR + NP, :, :, :], 1.0), sig=setup_dve)
        pool.do(lambda e: e.memset(mhalf_sb[:, :], -0.5), sig=setup)
        ev_setup = pool.do(lambda e: e.memset(v_sb[:, :, :, :], 1.0), sig=setup)
        ev_wv = dve.do(lambda e: e.tensor_scalar(wv_sb[:, :, :], wv_sb[:, :, :], 0.25, None, ALU.mult),
                       after=[ev_const], sig=setup_dve)
        for q in (pe, act, dve, pool):
            q.wait(ev_const, ev_setup)
        pe.wait(ev_wv)

        free = {}

        def freed(*names):
            return [e for n in names for e in free.get(n, ())]

        def layernorm(b, c, s):
            r = b % XR
            ev = None
            for t in range(CT):
                tile = c * CT + t
                ev = dve.do(lambda e, t=t, tile=tile: e.bn_stats(st_sb[:, s, t, :], x_sb[:, r, tile, :]),
                            after=[x_ready[b, c]], sig=dve_dense)
            for t in range(CT):
                ev2 = dve.do(lambda e, t=t: e.bn_aggr(mv_sb[:, s, t, :], st_sb[:, s, t, :]),
                             after=[ev] + freed(("mv", s)), sig=dve_dense)
            ev = pool.do(lambda e: e.tensor_scalar(rs_sb[:, s, :], mv_sb[:, s, :, 1], EPS, None, ALU.add),
                         after=[ev2] + freed(("mv", s)), sig=pool_dense)
            ev = pool.do(lambda e: e.tensor_tensor(rs_sb[:, s, :], rs_sb[:, s, :], mhalf_sb[:, :], ALU.pow),
                         after=[ev], sig=pool_dense)
            for t in range(CT):
                tile = c * CT + t
                e3 = pool.do(lambda e, t=t, tile=tile: e.tensor_scalar(
                    xt_sb[:, s, t, :], x_sb[:, r, tile, :], mv_sb[:, s, t, 0:1], rs_sb[:, s, t:t + 1],
                    ALU.subtract, ALU.mult), after=[ev] + freed(("xt", s)), sig=pool_dense)
            free["mv", s] = [e3]
            return e3

        def transposed(s, ev_xt, ev_carry=None):
            pe.wait(ev_xt, *freed("ps_d"))
            for cc in range(CC):
                for t in range(CT):
                    last = (cc, t) == (CC - 1, CT - 1)
                    ev = pe.do(lambda e, cc=cc, t=t: e.transpose(
                        ps_d[:, cc * CH + t * P:cc * CH + (t + 1) * P], xt_sb[:, s, t, cc * P:(cc + 1) * P],
                        id_sb[:, :]), sig=pe_dense if last else None)
            free["xt", s] = [ev]
            e2 = act.do(lambda e: e.activation(xn_sb[:, s, :, 1:CH + 1],
                                               ps_d[:, :].rearrange("p (c n) -> p c n", c=CC), ACT.Copy),
                        after=[ev, ev_carry] + freed(("xn", s)), sig=act_dense)
            free["ps_d"] = [e2]
            return e2

        def product(parts, after):
            pe.wait(*after, *freed("ps_d"))
            for n, (cols, pairs) in enumerate(parts):
                for k, (l, r) in enumerate(pairs):
                    last = n == len(parts) - 1 and k == len(pairs) - 1
                    ev = pe.do(lambda e, cols=cols, l=l, r=r, k=k, m=len(pairs): e.matmul(
                        ps_d[:, cols], l, r, start=(k == 0), stop=(k == m - 1)), sig=pe_dense if last else None)
            return ev

        def halves(n):
            return slice(n * CH, (n + 1) * CH)

        def ffn_chunk(b, c, s):
            r = b % XR
            ev_xt = layernorm(b, c, s)
            yield
            src = xn_sb[:, s, :, CH:CH + 1]
            if c == 0:
                ev_carry = pool.do(lambda e: e.memset(xn_sb[:, s, :, 0:1], 0.0), after=freed(("xn", s)), sig=pool_dense)
            else:
                ev_carry = pool.do(lambda e: e.tensor_copy(xn_sb[:, s, :, 0:1], src), after=freed(("xn", s)),
                                   sig=pool_dense)
            ev_xn = transposed(s, ev_xt, ev_carry)
            yield
            cur, prev = xn_sb[:, s, :, 1:CH + 1], xn_sb[:, s, :, 0:CH]
            ev_d = pool.do(lambda e: e.tensor_tensor(dif_sb[:, s, :, :], cur, prev, ALU.subtract),
                           after=[ev_xn, ev_carry] + freed(("dif", s)), sig=pool_dense)
            for dst, mu, name in ((xk_sb, muk_sb, "xk"), (dif_sb, mur_sb, "dif")):
                for cc in range(CC):
                    ev = dve.do(lambda e, cc=cc, dst=dst, mu=mu: e.scalar_tensor_tensor(
                        out=dst[:, s, cc, :], in0=dif_sb[:, s, cc, :], scalar=mu[:, cc:cc + 1],
                        in1=xn_sb[:, s, cc, 0:CH], op0=ALU.mult, op1=ALU.add),
                        after=[ev_d, dve_dense.now()] + freed((name, s)), sig=dve_dense)
                if name == "xk":
                    ev_xk = ev
            ev_xr = ev
            free["xn", s] = [ev_xr, ev_d]
            yield
            ev = product([(halves(m), [(wk_sb[:, cc, m * P:(m + 1) * P], xk_sb[:, s, cc, :]) for cc in range(CC)])
                          for m in range(CC)], [ev_xk])
            free["xk", s] = [ev]
            ev_relu = act.do(lambda e: e.activation(ka_sb[:, s, :, :], ps_d[:, :].rearrange("p (c n) -> p c n", c=CC),
                                                    ACT.Relu), after=[ev] + freed(("ka", s)), sig=act_dense)
            free["ps_d"] = [ev_relu]
            ev_ka = pool.do(lambda e: e.tensor_tensor(ka_sb[:, s, :, :], ka_sb[:, s, :, :], ka_sb[:, s, :, :], ALU.mult),
                            after=[ev_relu], sig=pool_dense)
            yield
            ev = product([(halves(t), [(dif_sb[:, s, cc, t * P:(t + 1) * P], wr_sb[:, cc, :]) for cc in range(CC)])
                          for t in range(CT)], [ev_xr])
            free["dif", s] = [ev]
            ev_th = act.do(lambda e: e.activation(xt_sb[:, s, :, :], ps_d[:, :].rearrange("p (t n) -> p t n", t=CT),
                                                  ACT.Tanh, scale=0.5), after=[ev] + freed(("xt", s)), sig=act_dense)
            free["ps_d"] = [ev_th]
            yield
            ev = product([(halves(t), [(ka_sb[:, s, cc, t * P:(t + 1) * P], wv_sb[:, cc, :]) for cc in range(CC)])
                          for t in range(CT)], [ev_ka])
            free["ka", s] = [ev]
            ev_u = dve.do(lambda e: e.scalar_tensor_tensor(
                out=xt_sb[:, s, :, :], in0=xt_sb[:, s, :, :], scalar=1.0,
                in1=ps_d[:, :].rearrange("p (t n) -> p t n", t=CT), op0=ALU.add, op1=ALU.mult),
                after=[ev, ev_th], sig=dve_dense)
            free["ps_d"] = [ev_u]
            xc = x_sb[:, r, c * CT:(c + 1) * CT, :]
            x_ready[b, c] = pool.do(lambda e: e.tensor_tensor(xc, xc, xt_sb[:, s, :, :], ALU.add),
                                    after=[ev_u, x_ready[b, c]], sig=pool_dense)
            free["xt", s] = [x_ready[b, c]]
            yield

        def qkv_chunk(b, c, s):
            ev_xt = layernorm(b, c, s)
            yield
            ev_xn = transposed(s, ev_xt)
            yield
            qk = []
            for n in range(2):
                ev = product([(halves(m), [(wqk_sb[:, cc, (2 * n + m) * P:(2 * n + m + 1) * P],
                                            xn_sb[:, s, cc, 1:CH + 1]) for cc in range(CC)]) for m in range(2)], [ev_xn])
                for m in range(2):
                    eb = act.do(lambda e, m=m, n=n: e.activation(
                        qb_sb[:, n, m, :], ps_d[:, halves(m)], ACT.Identity, bias=bqk_sb[:, 2 * n + m:2 * n + m + 1]),
                        after=[ev] + freed(("qb", n)), sig=act_dense)
                free["ps_d"] = [eb]
                sp.wait(eb, *freed(("sw", n)))
                for q in range(4):
                    es = sp.do(lambda e, n=n, q=q: e.dma_start(
                        sw_sb[32 * q:32 * q + 32, n, :, :], qb_sb[32 * (q ^ 1):32 * (q ^ 1) + 32, n, :, :]),
                        sig=swapped[n], by=16)
                qk.append((eb, es))
                yield
            ev = product([(halves(t), [(xn_sb[:, s, cc, 1 + t * P:1 + (t + 1) * P], wvv_sb[:, cc, :])
                                       for cc in range(CC)]) for t in range(CT)], [ev_xn])
            free["xn", s] = [ev]
            for t in range(CT):
                dst = v_sb[:, b % 2, c * CT + t, 0:H * VW].rearrange("p (h w) -> p h w", w=VW)[:, :, 0:HS]
                ev2 = dve.do(lambda e, t=t, dst=dst: e.tensor_tensor(
                    dst, ps_d[:, halves(t)].rearrange("p (h d) -> p h d", d=HS),
                    bv_sb[:, :].rearrange("p (h d) -> p h d", d=HS), ALU.add),
                    after=[ev] + freed(("v", b % 2)), sig=dve_dense)
            free["ps_d"] = [ev2]
            v_ready[b] = ev2
            cols = slice(c * CH, (c + 1) * CH)
            for n in range(2):
                eb, es = qk[n]
                cos = cos_sb[:, cols].rearrange("p (o n) -> p o n", o=1).broadcast_to([P, 2, CH])
                sin = sin_sb[:, cols].rearrange("p (o n) -> p o n", o=1).broadcast_to([P, 2, CH])
                q, w = qb_sb[:, n, :, :], sw_sb[:, n, :, :]
                e1 = pool.do(lambda e, q=q, cos=cos: e.tensor_tensor(q, q, cos, ALU.mult), after=[eb, es], sig=pool_dense)
                e2 = dve.do(lambda e, w=w, sin=sin: e.tensor_tensor(w, w, sin, ALU.mult), after=[es], sig=dve_dense)
                yield
                e3 = dve.do(lambda e, q=q, w=w: e.tensor_tensor(q, q, w, ALU.add), after=[e1, e2], sig=dve_dense)
                free["sw", n] = [e3]
                part = [part_sb[:, i, 2 * n:2 * n + 2, cols] for i in range(NP)]
                e4 = act.do(lambda e, q=q, p=part: e.activation(p[0], q, ACT.Copy),
                            after=[e3] + freed("part"), sig=act_dense)
                e5 = pool.do(lambda e, q=q, p=part: e.tensor_tensor(q, q, p[0], ALU.subtract), after=[e4], sig=pool_dense)
                yield
                e6 = act.do(lambda e, q=q, p=part: e.activation(p[1], q, ACT.Copy), after=[e5], sig=act_dense)
                e7 = pool.do(lambda e, q=q, p=part: e.tensor_tensor(p[2], q, p[1], ALU.subtract), after=[e6],
                             sig=pool_dense)
                free["qb", n] = [e7]
                parts_ready[b] = parts_ready.get(b, []) + [e4, e6, e7]
                yield

        def proj_chunk(b, c):
            r = b % XR
            ev = product([(halves(t), [(yn_sb[:, g, (c * CT + t) * P:(c * CT + t + 1) * P], wp_sb[:, g, :])
                                       for g in range(NG)]) for t in range(CT)], y_ready[b])
            free["yn"] = [ev]
            xc = x_sb[:, r, c * CT:(c + 1) * CT, :]
            x_ready[b, c] = dve.do(lambda e: e.tensor_tensor(
                xc, xc, ps_d[:, :].rearrange("p (t n) -> p t n", t=CT), ALU.add),
                after=[ev, x_ready[b, c]], sig=dve_dense)
            free["ps_d"] = [x_ready[b, c]]
            yield

        def before_attention(b):
            for c in range(NCH):
                yield from ffn_chunk(b, c, 0)
            for c in range(NCH):
                yield from qkv_chunk(b, c, 0)

        def after_attention(b):
            for c in range(NCH):
                yield from proj_chunk(b, c)
            for c in range(NCH):
                yield from ffn_chunk(b, c, 1)
                r = b % XR
                dst = out[b].rearrange("(t p) c -> p t c", p=P)[:, c * CT:(c + 1) * CT, :]
                sp.do(lambda e, c=c, r=r, dst=dst: e.dma_start(dst, x_sb[:, r, c * CT:(c + 1) * CT, :]),
                      after=[x_ready[b, c]], sig=x_out[r][c], by=16)
                if b + XR < nb:
                    x_ready[b + XR, c] = load_x(b + XR, c)

        v_ready, parts_ready, y_ready = {}, {}, {}
        rows_ready, mrows_ready = {}, {}
        count = {"score": 0, "maxs": 0, "tick": 0, "y": 0}

        def gather_rows(n):
            b, g = divmod(n, NG)
            slot, m, base = n % 2, g // 2, 64 * (g % 2)
            sp.wait(*parts_ready[b], *freed(("rows", slot)))
            for dst, tile, terms in ((kr_sb, 2 + m, TERMS_K), (qr_sb, m, TERMS_Q)):
                for t, part in enumerate(terms):
                    ev = sp.do(lambda e, dst=dst, tile=tile, t=t, part=part: e.dma_start(
                        dst[t * HS:(t + 1) * HS, slot, :, :], part_sb[base:base + 64, part, tile, :]),
                        sig=rows_in[slot], by=16)
            rows_ready[n] = ev
            if g == NG - 1:
                free["part"] = [ev]

        def max_units(n):
            slot = n % 2
            for i in range(TT):
                for j in range(G):
                    u = count["maxs"]
                    count["maxs"] += 1
                    width = (i + 1) * P
                    pe.wait(rows_ready[n], *freed(("ps_m", u % 2)))
                    for k0 in range(0, width, QC):
                        k1 = min(width, k0 + QC)
                        ev = pe.do(lambda e, u=u, i=i, j=j, k0=k0, k1=k1: e.matmul(
                            ps_m[:, u % 2, k0:k1], qr_sb[0:KR, slot, j, i * P:(i + 1) * P],
                            kr_sb[0:KR, slot, j, k0:k1], start=True, stop=True),
                            sig=pe_maxs if k1 == width else None)
                    e2 = dve.do(lambda e, u=u, i=i, j=j, width=width: e.tensor_tensor_reduce(
                        junk_sb[:, 0:width], ps_m[:, u % 2, 0:width], mask_sb[:, T - width:T], 1.0, -3e38,
                        ALU.add, ALU.max, mx_sb[:, slot, j * TT + i:j * TT + i + 1]),
                        after=[ev, dve_max.now()] + freed(("mx", slot)), sig=dve_max)
                    free["ps_m", u % 2] = [e2]
                    yield
            hi, mid, lo = (mp_sb[:, slot, i, :] for i in range(NP))
            e1 = dve.do(lambda e: e.tensor_scalar(hi, mx_sb[:, slot, :], -1.0, None, ALU.mult),
                        after=[dve_max.now()] + freed(("mp", slot)), sig=dve_max)
            e1 = dve.do(lambda e: e.scalar_tensor_tensor(out=mres_sb[:, slot, :], in0=mx_sb[:, slot, :], scalar=-1.0,
                                                         in1=hi, op0=ALU.mult, op1=ALU.subtract), after=[e1], sig=dve_max)
            free["mx", slot] = [e1]
            e1 = dve.do(lambda e: e.tensor_copy(mid, mres_sb[:, slot, :]), after=[e1], sig=dve_max)
            ev_mp = dve.do(lambda e: e.tensor_tensor(lo, mres_sb[:, slot, :], mid, ALU.subtract), after=[e1], sig=dve_max)
            yield
            nrow = NP * G * TT
            mt_ps = ps_d[:, 0:P // 2].bitcast(BF16)
            ev = pe.do(lambda e: e.transpose(mt_ps[0:nrow, :], mp_sb[:, slot, :, :].rearrange("p i n -> p (i n)"),
                                             idb_sb[:, :]), after=[ev_mp] + freed("ps_d"), sig=pe_dense)
            free["mp", slot] = [ev]
            e2 = act.do(lambda e: e.activation(mt_sb[0:nrow, slot, :], mt_ps[0:nrow, :], ACT.Copy),
                        after=[ev] + freed(("mt", slot)), sig=act_dense)
            free["ps_d"] = [e2]
            for i in range(NP):
                e3 = sp.do(lambda e, i=i: e.dma_start(
                    qr_sb[KR + i:KR + i + 1, slot, :, :].rearrange("o j (i q) -> o (j i) q", q=P),
                    mt_sb[i * G * TT:(i + 1) * G * TT, slot, :]), after=[e2] + freed(("rows", slot)), sig=mrows_in[slot], by=16)
            free["mt", slot] = [e3]
            mrows_ready[n] = e3
            yield

        def normalise(b, g, qc, ev_pv):
            k = count["y"] % 2
            count["y"] += 1
            e1 = act.do(lambda e: e.activation(yt_sb[:, k, :], ps_y[:, :], ACT.Copy), after=[ev_pv] + freed(("yt", k)),
                        sig=act_dense)
            free["ps_y"] = [e1]

            def later():
                e2 = dve.do(lambda e: e.stream_shuffle(den_sb[:, k, :], yt_sb[:, k, :], [HS] * 32),
                            after=[e1] + freed(("den", k)), sig=dve_dense)
                e2 = dve.do(lambda e: e.reciprocal(den_sb[:, k, :], den_sb[:, k, :]), after=[e2], sig=dve_dense)
                e3 = pool.do(lambda e: e.tensor_tensor(yn_sb[:, g, qc * QC:(qc + 1) * QC], yt_sb[:, k, :],
                                                       den_sb[:, k, :], ALU.mult), after=[e2] + freed("yn"), sig=pool_dense)
                free["yt", k] = free["den", k] = [e3]
                y_ready[b] = [e3]
            return later

        def pv(tick):
            b, g, qc, kb, width, buf, ready = tick
            last_kb = KQ * (qc + 1) - 1
            pe.wait(ready, v_ready[b])
            if kb == 0:
                pe.wait(*freed("ps_y"))
            for j in range(G):
                col = (G * g + j) * VW
                ev = pe.do(lambda e, j=j, col=col: e.matmul(
                    ps_y[32 * j:32 * j + 32, QC - width:QC], v_sb[:, b % 2, kb, col:col + 32],
                    pt_sb[:, buf, j, 0:width], start=(kb == 0), stop=(kb == last_kb)),
                    sig=pe_pv if j == G - 1 else None)
            free["pt", buf] = [ev]
            free["v", b % 2] = [ev]
            if kb == last_kb:
                return normalise(b, g, qc, ev)
            return None

        def run(gen, n):
            for _ in range(n):
                if gen is None or next(gen, "end") == "end":
                    return

        def attention_tick(n, qc, kb, before, fill_max, fill_dense):
            b, g = divmod(n, NG)
            slot = n % 2
            buf = count["tick"] % 2
            count["tick"] += 1
            skip = max(0, kb - KQ * qc) * P
            width = QC - skip
            q0 = qc * QC + skip
            later = None
            evs = []
            for j in range(G):
                u = count["score"]
                count["score"] += 1
                ev = pe.do(lambda e, j=j, u=u: e.matmul(
                    ps_s[:, u % 2, 0:width], kr_sb[0:KR + NP, slot, j, kb * P:(kb + 1) * P],
                    qr_sb[0:KR + NP, slot, j, q0:q0 + width], start=True, stop=True),
                    after=[rows_ready[n], mrows_ready[n]] + freed(("ps_s", u % 2)), sig=pe_score)
                e2 = act.do(lambda e, j=j, u=u: e.activation(pt_sb[:, buf, j, 0:width], ps_s[:, u % 2, 0:width],
                                                             ACT.Exp, scale=SCALE),
                            after=[ev] + freed(("pt", buf)), sig=act_exp)
                free["ps_s", u % 2] = [e2]
                if j == 1:
                    fill_max(0)
                if j == 2:
                    if before is not None:
                        later = pv(before)
                    fill_dense()
            free["rows", slot] = [ev]
            ready = e2
            if kb >= KQ * qc:
                diag = pt_sb[:, buf, :, 0:P]
                ready = pool.do(lambda e: e.affine_select(out=diag, in_=diag, compare_op=ALU.is_ge, fill=0.0, base=0,
                                                          pattern=[[0, G], [1, P]], channel_multiplier=-1),
                                after=[e2], sig=pool_mask)
            fill_max(1)
            return (b, g, qc, kb, width, buf, ready), later

        run(before_attention(0), 10 ** 6)
        gather_rows(0)
        run(max_units(0), 10 ** 6)

        n_groups = nb * NG
        ticks = [(qc, kb) for qc in range(NQC) for kb in range(KQ * (qc + 1))]
        NTK = len(ticks)
        before, later = None, None
        for b in range(nb):
            pre = before_attention(b + 1) if b + 1 < nb else None
            post = after_attention(b - 1) if b > 0 else None
            n_pre, n_post = NCH * 6 + NCH * 9, NCH + NCH * 6
            done_pre = done_post = 0
            for g in range(NG):
                n = b * NG + g
                nxt = None
                for k, (qc, kb) in enumerate(ticks):
                    at = g * NTK + k
                    if k == 1 and n + 1 < n_groups:
                        nxt = max_units(n + 1)

                    def fill_max(half, k=k, nxt=None):
                        pass

                    want = 0 if nxt is None else -(-(G * TT) * min(k, NTK - 3) // (NTK - 3))
                    state = {"nxt": nxt, "k": k}

                    def fill_max(half, k=k, nxt=nxt):
                        if nxt is None:
                            return
                        if k <= NTK - 3:
                            lo, hi = (G * TT * (k - 1)) // (NTK - 3), (G * TT * k) // (NTK - 3)
                            mid = (lo + hi) // 2
                            run(nxt, (mid - lo) if half == 0 else (hi - mid))
                        elif k == NTK - 2:
                            run(nxt, 1)

                    def fill_dense(at=at):
                        nonlocal done_pre, done_post
                        goal = min(at + 1, NCH) + max(0, min(NCH * 6, NCH * 6 * (at + 1 - NCH) // (NG * NTK - 2 - NCH)))
                        run(post, goal - done_post)
                        done_post = goal
                        half = (NG - 2) * NTK
                        goal = NCH * 6 * min(at + 1, half) // half
                        if at + 1 > half:
                            goal += min(NCH * 9, NCH * 9 * (at + 1 - half) // (NTK - 1))
                        run(pre, goal - done_pre)
                        done_pre = goal

                    if k == 0 and n + 1 < n_groups:
                        if g == NG - 1:
                            run(pre, 10 ** 6)
                        gather_rows(n + 1)
                    tick, nl = attention_tick(n, qc, kb, before, fill_max, fill_dense)
                    if later is not None:
                        later()
                    before, later = tick, nl
                if nxt is not None:
                    run(nxt, 10 ** 6)
            run(post, 10 ** 6)
            run(pre, 10 ** 6)
        later2 = pv(before)
        if later is not None:
            later()
        later2()
        run(after_attention(nb - 1), 10 ** 6)
        for r in range(XR):
            for c in range(NCH):
                sp.wait(x_out[r][c].now())

        block = ctx.enter_context(nc.Block())

        @block.tensor
        def _(eng):
            pe.play(eng)

        @block.scalar
        def _(eng):
            act.play(eng)

        @block.vector
        def _(eng):
            dve.play(eng)

        @block.gpsimd
        def _(eng):
            pool.play(eng)

        @block.sync
        def _(eng):
            sp.play(eng)


def rope_tables():
    pos = np.arange(T, dtype=np.float32)[:, None]
    i = np.arange(1, HS // 2 + 1, dtype=np.float32)[None]
    theta = (np.float32(1.0) / np.float32(10000.0) ** (np.float32(2.0) * (i - np.float32(1.0)) / np.float32(HS))).astype(np.float32)
    ang = (pos * theta).astype(np.float32)
    cos, sin = np.cos(ang).T, np.sin(ang).T
    signed = np.stack([-sin, sin])
    cos = np.broadcast_to(cos[None, None, :, None, :], (2, 2, HS // 2, G, T))
    signed = np.broadcast_to(signed[None, :, :, None, :], (2, 2, HS // 2, G, T))
    return (np.ascontiguousarray(cos.reshape(P, T), dtype=np.float32),
            np.ascontiguousarray(signed.reshape(P, T), dtype=np.float32))


def kernel(L0_attn_x, L0_attn_W_qkv, L0_attn_b_qkv, L0_attn_W_proj, L0_attn_b_proj, L0_ffn_W_r, L0_ffn_W_k,
           L0_ffn_W_v, L0_ffn_mu_r, L0_ffn_mu_k):
    import concourse.bacc as bacc
    from concourse.bass_utils import run_bass_kernel_spmd

    x = np.ascontiguousarray(L0_attn_x)
    w = np.asarray(L0_attn_W_qkv).reshape(C, 2, 2, G, 3, HS // 2, 2)
    bq = np.asarray(L0_attn_b_qkv).reshape(2, 2, G, 3, HS // 2, 2)
    w_qk = w[:, :, :, :, 0:2].transpose(0, 4, 1, 2, 6, 5, 3).reshape(C, 2 * C)
    b_qk = bq[:, :, :, 0:2].transpose(3, 0, 1, 5, 4, 2).reshape(4, P).T
    w_v = np.asarray(L0_attn_W_qkv).reshape(C, H, 3, HS)[:, :, 2].reshape(C, C)
    b_v = np.asarray(L0_attn_b_qkv).reshape(H, 3, HS)[:, 2].reshape(1, C)
    rope_c, rope_s = rope_tables()
    arrays = {
        "x": x,
        "w_r": np.asarray(L0_ffn_W_r).T, "w_k": np.asarray(L0_ffn_W_k).T, "w_v": np.asarray(L0_ffn_W_v).T,
        "mu_r": np.asarray(L0_ffn_mu_r).reshape(CC, P).T, "mu_k": np.asarray(L0_ffn_mu_k).reshape(CC, P).T,
        "w_qk": w_qk, "b_qk": b_qk, "w_vv": w_v, "b_v": b_v,
        "w_p": np.asarray(L0_attn_W_proj), "b_p": np.asarray(L0_attn_b_proj).reshape(1, C),
        "rope_c": rope_c, "rope_s": rope_s,
    }
    arrays = {n: np.ascontiguousarray(a) for n, a in arrays.items()}
    nc = bacc.Bacc("TRN2", target_bir_lowering=False, num_devices=1)
    aps = {n: nc.dram_tensor(n, a.shape, mybir.dt.from_np(a.dtype), kind="ExternalInput").ap() for n, a in arrays.items()}
    out = nc.dram_tensor("out", x.shape, mybir.dt.from_np(x.dtype), kind="ExternalOutput").ap()
    macaron(nc, out=out, nb=x.shape[0], **aps)
    r = run_bass_kernel_spmd(nc, [arrays], core_ids=[0])
    return r.results[0]["out"]
```

```python
from contextlib import ExitStack

import numpy as np

import concourse.bass as bass
import concourse.mybir as mybir

F32 = mybir.dt.float32
BF16 = mybir.dt.bfloat16
ALU = mybir.AluOpType
ACT = mybir.ActivationFunctionType

P = 128
B, T, C = 16, 1024, 256
H, HS = 16, 16
EPS = 1e-5
CC = C // P
TT = T // P
CH = 256
CT = CH // P
NCH = T // CH
G = 4
NG = H // G
QC = 512
NQC = T // QC
KQ = QC // P
TERMS_Q = (0, 0, 0, 1, 1, 2)
TERMS_K = (0, 1, 2, 0, 1, 0)
NT = len(TERMS_Q)
KR = NT * HS
NP = 3
VW = HS + 1
VPAD = 32 - VW
NEG = -1e30
SCALE = HS ** -0.5


class Event:
    def __init__(self, sem, value):
        self.sem, self.value = sem, value


class Counter:

    def __init__(self, sem):
        self.sem, self.value = sem, 0

    def bump(self, by):
        self.value += by
        return Event(self, self.value)

    def now(self):
        return Event(self, self.value)


class Queue:

    def __init__(self):
        self.ops, self.reached = [], {}

    def wait(self, *events):
        for e in events:
            if e is not None and self.reached.get(e.sem, 0) < e.value:
                self.reached[e.sem] = e.value
                self.ops.append(lambda eng, s=e.sem.sem, v=e.value: eng.wait_ge(s, v))

    def do(self, make, after=(), sig=None, by=1):
        self.wait(*after)
        if sig is None:
            self.ops.append(make)
            return None
        self.ops.append(lambda eng, s=sig.sem: make(eng).then_inc(s, by))
        return sig.bump(by)

    def play(self, eng):
        for op in self.ops:
            op(eng)


def macaron(nc, x, w_r, w_k, w_v, mu_r, mu_k, w_qk, b_qk, w_vv, b_v, w_p, b_p, rope_c, rope_s, out, nb=B):
    ctx = ExitStack()
    with ctx:
        def sb(name, shape, dt=F32):
            return ctx.enter_context(nc.sbuf_tensor(name, shape, dt))

        def counter(name):
            return Counter(ctx.enter_context(nc.semaphore(name)))

        NS, NM, ND = 2, 3, 2
        XR = 3
        RS = 3
        x_sb = sb("x_sb", [P, XR, TT, C])
        xt_sb = sb("xt_sb", [P, 2, CT, C])
        xn_sb = sb("xn_sb", [P, 2, CC, CH + 1])
        dif_sb = sb("dif_sb", [P, 2, CC, CH])
        xk_sb = sb("xk_sb", [P, CC, CH])
        ka_sb = sb("ka_sb", [P, 2, CC, CH])
        st_sb = sb("st_sb", [P, 2, CT, 6])
        mv_sb = sb("mv_sb", [P, 2, CT, 2])
        rs_sb = sb("rs_sb", [P, 2, CT])
        mhalf_sb = sb("mhalf_sb", [P, CT])
        qb_sb = sb("qb_sb", [P, 2, 2, CH])
        sw_sb = sb("sw_sb", [P, 2, 2, CH])
        part_sb = sb("part_sb", [P, NP, 4, T], BF16)
        v_sb = sb("v_sb", [P, 2, TT, H * VW + VPAD])
        qr_sb = sb("qr_sb", [P, RS, G, T], BF16)
        kr_sb = sb("kr_sb", [P, RS, G, T], BF16)
        pt_sb = sb("pt_sb", [P, 2, G, QC])
        yt_sb = sb("yt_sb", [P, 2, QC])
        den_sb = sb("den_sb", [P, 2, G * QC // P])
        rden_sb = sb("rden_sb", [P, QC])
        yn_sb = sb("yn_sb", [P, NG, T])
        mx_sb = sb("mx_sb", [P, 2, 2, G * TT])
        mres_sb = sb("mres_sb", [P, 2, G * TT])
        mp_sb = sb("mp_sb", [P, 2, NP, G * TT], BF16)
        mt_sb = sb("mt_sb", [P, 2, P], BF16)
        wr_sb = sb("wr_sb", [P, CC, C])
        wk_sb = sb("wk_sb", [P, CC, C])
        wv_sb = sb("wv_sb", [P, CC, C])
        wqk_sb = sb("wqk_sb", [P, CC, 2 * C])
        wvv_sb = sb("wvv_sb", [P, CC, C])
        wp_sb = sb("wp_sb", [P, NG, C])
        mur_sb = sb("mur_sb", [P, CC])
        muk_sb = sb("muk_sb", [P, CC])
        bqk_sb = sb("bqk_sb", [P, 4])
        bv_sb = sb("bv_sb", [P, C])
        cos_sb = sb("cos_sb", [P, T])
        sin_sb = sb("sin_sb", [P, T])
        mask_sb = sb("mask_sb", [P, 2, QC], BF16)
        id_sb = sb("id_sb", [P, P])
        idb_sb = sb("idb_sb", [P, P], BF16)

        ps_s = ctx.enter_context(nc.psum_tensor("ps_s", [P, NS, QC], F32))
        ps_m = ctx.enter_context(nc.psum_tensor("ps_m", [P, NM, QC], F32))
        ps_y = ctx.enter_context(nc.psum_tensor("ps_y", [P, QC], F32))
        ps_d = ctx.enter_context(nc.psum_tensor("ps_d", [P, ND, QC], F32))

        consts = counter("consts")
        x_in = [[counter(f"x_in{r}_{c}") for c in range(NCH)] for r in range(XR)]
        x_out = [[counter(f"x_out{r}_{c}") for c in range(NCH)] for r in range(XR)]
        swapped = [counter("swapped_q"), counter("swapped_k")]
        rows_in = [counter(f"rows_in{r}") for r in range(RS)]
        mrows_in = [counter(f"mrows_in{r}") for r in range(RS)]
        den_out = [counter("den_out0"), counter("den_out1")]
        den_in = [counter("den_in0"), counter("den_in1")]
        pe_score = counter("pe_score")
        pe_maxs = counter("pe_maxs")
        pe_pv = counter("pe_pv")
        pe_dense = counter("pe_dense")
        act_exp = counter("act_exp")
        act_dense = counter("act_dense")
        dve_max = counter("dve_max")
        dve_dense = counter("dve_dense")
        pool_mask = counter("pool_mask")
        pool_dense = counter("pool_dense")
        setup = counter("setup")
        setup_dve = counter("setup_dve")

        pe, act, dve, pool, sp = (Queue() for _ in range(5))

        def chunked(w):
            return w.rearrange("(c p) n -> p c n", p=P)

        ev_zero = pool.do(lambda e: e.memset(wp_sb[:, :, :], 0.0), sig=setup)
        const_loads = [
            (wr_sb[:, :, :], chunked(w_r)), (wk_sb[:, :, :], chunked(w_k)), (wv_sb[:, :, :], chunked(w_v)),
            (wqk_sb[:, :, :], chunked(w_qk)), (wvv_sb[:, :, :], chunked(w_vv)),
            (mur_sb[:, :], mu_r), (muk_sb[:, :], mu_k), (bqk_sb[:, :], b_qk),
            (bv_sb[:, :], b_v.broadcast_to([P, C])), (cos_sb[:, :], rope_c), (sin_sb[:, :], rope_s),
        ]

        def load_x(b, c):
            r = b % XR
            src = x[b].rearrange("(t p) c -> p t c", p=P)[:, c * CT:(c + 1) * CT, :]
            return sp.do(lambda e: e.dma_start(x_sb[:, r, c * CT:(c + 1) * CT, :], src),
                         after=[x_out[r][c].now()], sig=x_in[r][c], by=16)

        x_ready = {}
        for c in range(NCH):
            x_ready[0, c] = load_x(0, c)
        for dst, src in const_loads:
            sp.do(lambda e, d=dst, s=src: e.dma_start(d, s), sig=consts, by=16)
        sp.wait(ev_zero)
        for g in range(NG):
            for j in range(G):
                h = G * g + j
                sp.do(lambda e, g=g, j=j, h=h: e.dma_start(wp_sb[32 * j:32 * j + HS, g, :], w_p[h * HS:(h + 1) * HS, :]),
                      sig=consts, by=16)
        sp.do(lambda e: e.dma_start(wp_sb[HS:HS + 1, 0, :], b_p), sig=consts, by=16)
        ev_const = consts.now()
        for b in range(1, min(nb, XR)):
            for c in range(NCH):
                x_ready[b, c] = load_x(b, c)

        pool.do(lambda e: e.memset(id_sb[:, :], 0.0), sig=setup)
        pool.do(lambda e: e.memset(idb_sb[:, :], 0.0), sig=setup)
        ev_mz = pool.do(lambda e: e.memset(mask_sb[:, :, :], 0.0), sig=setup)
        pool.wait(ev_mz)
        for t in (id_sb, idb_sb):
            pool.do(lambda e, t=t: e.affine_select(out=t[:, :], in_=t[:, :], compare_op=ALU.not_equal, fill=1.0,
                                                   base=0, pattern=[[-1, P]], channel_multiplier=1), sig=setup)
        pool.do(lambda e: e.affine_select(out=mask_sb[:, 1, QC - P:QC], in_=mask_sb[:, 1, QC - P:QC], compare_op=ALU.is_ge,
                                          fill=NEG, base=0, pattern=[[-1, P]], channel_multiplier=1), sig=setup)
        dve.do(lambda e: e.memset(rden_sb[:, :], 1.0), sig=setup_dve)
        ev_ones = dve.do(lambda e: e.memset(kr_sb[KR:KR + NP, :, :, :], 1.0), sig=setup_dve)
        pool.do(lambda e: e.memset(mhalf_sb[:, :], -0.5), sig=setup)
        ev_setup = pool.do(lambda e: e.memset(v_sb[:, :, :, :], 1.0), sig=setup)
        ev_wv = dve.do(lambda e: e.tensor_scalar(wv_sb[:, :, :], wv_sb[:, :, :], 0.25, None, ALU.mult),
                       after=[ev_const], sig=setup_dve)
        for q in (pe, act, dve, pool):
            q.wait(ev_const, ev_setup, ev_ones)
        pe.wait(ev_wv)
        sp.wait(ev_ones)

        count = {"score": 0, "maxs": 0, "tick": 0, "y": 0, "dense": 0}
        done = {}

        def last(*step):
            return done.get(step)

        def layernorm(b, c, s):
            r = b % XR
            for t in range(CT):
                ev = dve.do(lambda e, t=t: e.bn_stats(st_sb[:, s, t, :], x_sb[:, r, c * CT + t, :]),
                            after=[x_ready[b, c]], sig=dve_dense)
            for t in range(CT):
                ev_mv = dve.do(lambda e, t=t: e.bn_aggr(mv_sb[:, s, t, :], st_sb[:, s, t, :]),
                               after=[ev, last("rstd", s)], sig=dve_dense)
            yield
            ev = pool.do(lambda e: e.tensor_scalar(rs_sb[:, s, :], mv_sb[:, s, :, 1], EPS, None, ALU.add),
                         after=[ev_mv, last("normed", s)], sig=pool_dense)
            done["rstd", s] = ev
            ev = pool.do(lambda e: e.tensor_tensor(rs_sb[:, s, :], rs_sb[:, s, :], mhalf_sb[:, :], ALU.pow),
                         after=[ev], sig=pool_dense)
            yield
            for t in range(CT):
                ev_xt = dve.do(lambda e, t=t: e.tensor_scalar(
                    xt_sb[:, s, t, :], x_sb[:, r, c * CT + t, :], mv_sb[:, s, t, 0:1], rs_sb[:, s, t:t + 1],
                    ALU.subtract, ALU.mult), after=[ev, last("transposed", s), last("x_added", s)], sig=dve_dense)
            done["normed", s] = ev_xt
            yield
            return ev_xt

        def next_bank():
            count["dense"] += 1
            return count["dense"] % ND

        def transposed(s, ev_xt, ev_carry=None):
            d = next_bank()
            pe.wait(ev_xt, last("dense_out", d))
            for cc in range(CC):
                for t in range(CT):
                    final = (cc, t) == (CC - 1, CT - 1)
                    ev = pe.do(lambda e, d=d, cc=cc, t=t: e.transpose(
                        ps_d[:, d, cc * CH + t * P:cc * CH + (t + 1) * P], xt_sb[:, s, t, cc * P:(cc + 1) * P],
                        id_sb[:, :]), sig=pe_dense if final else None)
            done["transposed", s] = ev
            e2 = act.do(lambda e, d=d: e.activation(xn_sb[:, s, :, 1:CH + 1],
                                               by_half(ps_d[:, d, :]), ACT.Copy),
                        after=[ev, ev_carry, last("mixed", s), last("carried", s), last("v_made", s)],
                        sig=act_dense)
            done["dense_out", d] = e2
            return e2

        def product(parts, after):
            d = next_bank()
            pe.wait(*after, last("dense_out", d))
            for n, (cols, pairs) in enumerate(parts):
                for k, (l, r) in enumerate(pairs):
                    final = n == len(parts) - 1 and k == len(pairs) - 1
                    ev = pe.do(lambda e, d=d, cols=cols, l=l, r=r, k=k, m=len(pairs): e.matmul(
                        ps_d[:, d, cols], l, r, start=(k == 0), stop=(k == m - 1)), sig=pe_dense if final else None)
            return ev, d

        def halves(n):
            return slice(n * CH, (n + 1) * CH)

        def by_half(ap):
            return ap.rearrange("p (t n) -> p t n", t=CT)

        last_xn = {}

        def ffn_chunk(b, c, s, finish=None):
            r = b % XR
            ev_xt = yield from layernorm(b, c, s)
            if c == 0:
                ev_carry = pool.do(lambda e: e.memset(xn_sb[:, s, :, 0:1], 0.0), after=[last("mixed", s)], sig=pool_dense)
            else:
                sp_, ev_prev = last_xn[b]
                ev_carry = pool.do(lambda e: e.tensor_copy(xn_sb[:, s, :, 0:1], xn_sb[:, sp_, :, CH:CH + 1]),
                                   after=[ev_prev, last("mixed", s)], sig=pool_dense)
                done["carried", sp_] = ev_carry
            ev_xn = transposed(s, ev_xt, ev_carry)
            last_xn[b] = (s, ev_xn)
            yield
            cur, prev = xn_sb[:, s, :, 1:CH + 1], xn_sb[:, s, :, 0:CH]
            ev_d = pool.do(lambda e: e.tensor_tensor(dif_sb[:, s, :, :], cur, prev, ALU.subtract),
                           after=[ev_xn, ev_carry, last("r_made", s)], sig=pool_dense)
            yield
            for cc in range(CC):
                ev_xk = dve.do(lambda e, cc=cc: e.scalar_tensor_tensor(
                    out=xk_sb[:, cc, :], in0=dif_sb[:, s, cc, :], scalar=muk_sb[:, cc:cc + 1],
                    in1=xn_sb[:, s, cc, 0:CH], op0=ALU.mult, op1=ALU.add), after=[ev_d, last("k_made")], sig=dve_dense)
            for cc in range(CC):
                ev_xr = dve.do(lambda e, cc=cc: e.scalar_tensor_tensor(
                    out=dif_sb[:, s, cc, :], in0=dif_sb[:, s, cc, :], scalar=mur_sb[:, cc:cc + 1],
                    in1=xn_sb[:, s, cc, 0:CH], op0=ALU.mult, op1=ALU.add), after=[ev_xk], sig=dve_dense)
            done["mixed", s] = ev_xr
            yield
            ev, d = product([(halves(m), [(wk_sb[:, cc, m * P:(m + 1) * P], xk_sb[:, cc, :]) for cc in range(CC)])
                          for m in range(CC)], [ev_xk])
            done["k_made",] = ev
            ev_relu = act.do(lambda e, d=d: e.activation(ka_sb[:, s, :, :], by_half(ps_d[:, d, :]), ACT.Relu),
                             after=[ev, last("kv_made", s)], sig=act_dense)
            done["dense_out", d] = ev_relu
            yield
            ev_ka = act.do(lambda e: e.activation(ka_sb[:, s, :, :], ka_sb[:, s, :, :], ACT.Square),
                           after=[ev_relu], sig=act_dense)
            ev, d = product([(halves(t), [(dif_sb[:, s, cc, t * P:(t + 1) * P], wr_sb[:, cc, :]) for cc in range(CC)])
                          for t in range(CT)], [ev_xr])
            done["r_made", s] = ev
            ev_th = act.do(lambda e, d=d: e.activation(xt_sb[:, s, :, :], by_half(ps_d[:, d, :]), ACT.Tanh, scale=0.5),
                           after=[ev, last("transposed", s)], sig=act_dense)
            done["dense_out", d] = ev_th
            yield
            ev, d = product([(halves(t), [(ka_sb[:, s, cc, t * P:(t + 1) * P], wv_sb[:, cc, :]) for cc in range(CC)])
                          for t in range(CT)], [ev_ka])
            done["kv_made", s] = ev
            ev_u = dve.do(lambda e, d=d: e.scalar_tensor_tensor(
                out=xt_sb[:, s, :, :], in0=xt_sb[:, s, :, :], scalar=1.0, in1=by_half(ps_d[:, d, :]),
                op0=ALU.add, op1=ALU.mult), after=[ev, ev_th], sig=dve_dense)
            done["dense_out", d] = ev_u
            yield
            xc = x_sb[:, r, c * CT:(c + 1) * CT, :]
            x_ready[b, c] = pool.do(lambda e: e.tensor_tensor(xc, xc, xt_sb[:, s, :, :], ALU.add),
                                    after=[ev_u, x_ready[b, c]], sig=pool_dense)
            done["x_added", s] = x_ready[b, c]
            if finish is not None:
                finish(b, c)
            yield

        FFN_STEPS = 10

        def qkv_chunk(b, c, s):
            ev_xt = yield from layernorm(b, c, s)
            ev_xn = transposed(s, ev_xt)
            yield
            biased, turned = [], []
            for n in range(2):
                ev, d = product([(halves(m), [(wqk_sb[:, cc, (2 * n + m) * P:(2 * n + m + 1) * P],
                                            xn_sb[:, s, cc, 1:CH + 1]) for cc in range(CC)]) for m in range(2)], [ev_xn])
                for m in range(2):
                    eb = act.do(lambda e, d=d, m=m, n=n: e.activation(
                        qb_sb[:, n, m, :], ps_d[:, d, halves(m)], ACT.Identity, bias=bqk_sb[:, 2 * n + m:2 * n + m + 1]),
                        after=[ev, last("low_made", n)], sig=act_dense)
                done["dense_out", d] = eb
                sp.wait(eb, last("turned", n))
                for q in range(4):
                    es = sp.do(lambda e, n=n, q=q: e.dma_start(
                        sw_sb[32 * q:32 * q + 32, n, :, :], qb_sb[32 * (q ^ 1):32 * (q ^ 1) + 32, n, :, :]),
                        sig=swapped[n], by=16)
                biased.append(eb)
                turned.append(es)
                yield
            ev, d = product([(halves(t), [(xn_sb[:, s, cc, 1 + t * P:1 + (t + 1) * P], wvv_sb[:, cc, :])
                                       for cc in range(CC)]) for t in range(CT)], [ev_xn])
            done["v_made", s] = ev
            for t in range(CT):
                dst = v_sb[:, b % 2, c * CT + t, 0:H * VW].rearrange("p (h w) -> p h w", w=VW)[:, :, 0:HS]
                v_ready[b] = dve.do(lambda e, d=d, t=t, dst=dst: e.tensor_tensor(
                    dst, ps_d[:, d, halves(t)].rearrange("p (h d) -> p h d", d=HS),
                    bv_sb[:, :].rearrange("p (h d) -> p h d", d=HS), ALU.add),
                    after=[ev, last("pv", b % 2)], sig=dve_dense)
            done["dense_out", d] = v_ready[b]
            yield
            cols = slice(c * CH, (c + 1) * CH)
            cos = cos_sb[:, cols].rearrange("p (o n) -> p o n", o=1).broadcast_to([P, 2, CH])
            sin = sin_sb[:, cols].rearrange("p (o n) -> p o n", o=1).broadcast_to([P, 2, CH])
            q = [qb_sb[:, n, :, :] for n in range(2)]
            w = [sw_sb[:, n, :, :] for n in range(2)]
            part = [[part_sb[:, i, 2 * n:2 * n + 2, cols] for i in range(NP)] for n in range(2)]
            ev1, ev2, ev3, ev4, ev5, ev6 = [{} for _ in range(6)]

            def turn(n):
                ev1[n] = pool.do(lambda e: e.tensor_tensor(q[n], q[n], cos, ALU.mult), after=[biased[n], turned[n]],
                                 sig=pool_dense)
                ev2[n] = dve.do(lambda e: e.tensor_tensor(w[n], w[n], sin, ALU.mult), after=[turned[n]], sig=dve_dense)

            def add(n):
                ev3[n] = dve.do(lambda e: e.tensor_tensor(q[n], q[n], w[n], ALU.add), after=[ev1[n], ev2[n]],
                                sig=dve_dense)
                done["turned", n] = ev3[n]

            def high(n):
                ev4[n] = act.do(lambda e: e.activation(part[n][0], q[n], ACT.Copy),
                                after=[ev3[n], last("all_gathered")], sig=act_dense)

            def rest(n):
                ev5[n] = pool.do(lambda e: e.tensor_tensor(q[n], q[n], part[n][0], ALU.subtract), after=[ev4[n]],
                                 sig=pool_dense)

            def middle(n):
                ev6[n] = act.do(lambda e: e.activation(part[n][1], q[n], ACT.Copy), after=[ev5[n]], sig=act_dense)

            def low(n):
                ev = pool.do(lambda e: e.tensor_tensor(part[n][2], q[n], part[n][1], ALU.subtract),
                             after=[ev6[n], last("all_gathered")], sig=pool_dense)
                done["low_made", n] = ev
                parts_ready[b] = parts_ready.get(b, []) + [ev4[n], ev6[n], ev]

            todo = [turn, add, high, rest, middle, low]
            for step in range(len(todo) + 1):
                if step < len(todo):
                    todo[step](0)
                if step > 0:
                    todo[step - 1](1)
                yield

        QKV_STEPS = 14

        def proj_chunk(b, c):
            r = b % XR
            ev, d = product([(halves(t), [(yn_sb[:, g, (c * CT + t) * P:(c * CT + t + 1) * P], wp_sb[:, g, :])
                                       for g in range(NG)]) for t in range(CT)], y_ready[b])
            done["projected",] = ev
            xc = x_sb[:, r, c * CT:(c + 1) * CT, :]
            x_ready[b, c] = dve.do(lambda e, d=d: e.tensor_tensor(xc, xc, by_half(ps_d[:, d, :]), ALU.add),
                                   after=[ev, x_ready[b, c]], sig=dve_dense)
            done["dense_out", d] = x_ready[b, c]
            yield

        def staggered(chunks, lag):
            active, started, progress = [], 0, lag
            while active or started < len(chunks):
                if progress >= lag and started < len(chunks):
                    active.append(chunks[started])
                    started, progress = started + 1, 0
                for g in list(active):
                    if next(g, "end") == "end":
                        active.remove(g)
                    else:
                        yield
                progress += 1

        def store(b, c):
            r = b % XR
            dst = out[b].rearrange("(t p) c -> p t c", p=P)[:, c * CT:(c + 1) * CT, :]
            sp.do(lambda e: e.dma_start(dst, x_sb[:, r, c * CT:(c + 1) * CT, :]), after=[x_ready[b, c]],
                  sig=x_out[r][c], by=16)
            if b + XR < nb:
                x_ready[b + XR, c] = load_x(b + XR, c)

        def first_ffn(b, alone=False):
            chunks = [ffn_chunk(b, c, c % 2 if alone else 0) for c in range(NCH)]
            return staggered(chunks, 5 if alone else FFN_STEPS)

        def qkv(b, alone=False):
            return staggered([qkv_chunk(b, c, c % 2 if alone else 0) for c in range(NCH)], 10)

        def second_ffn(b, alone=False):
            chunks = [ffn_chunk(b, c, c % 2 if alone else 1, store) for c in range(NCH)]
            return staggered(chunks, 5 if alone else FFN_STEPS)

        def projection(b):
            return staggered([proj_chunk(b, c) for c in range(NCH)], 1)

        v_ready, parts_ready, y_ready = {}, {}, {}
        rows_ready, mrows_ready = {}, {}

        def gather_rows(n):
            b, g = divmod(n, NG)
            slot, m, base = n % RS, g // 2, 64 * (g % 2)
            assert len(parts_ready[b]) == 6 * NCH
            sp.wait(*parts_ready[b], last("scores", slot))
            for dst, tile, terms in ((kr_sb, 2 + m, TERMS_K), (qr_sb, m, TERMS_Q)):
                for t, part in enumerate(terms):
                    ev = sp.do(lambda e, dst=dst, tile=tile, t=t, part=part: e.dma_start(
                        dst[t * HS:(t + 1) * HS, slot, :, :], part_sb[base:base + 64, part, tile, :]),
                        sig=rows_in[slot], by=16)
                    if t % 2:
                        yield
            rows_ready[n] = ev
            if g == NG - 1:
                done["all_gathered",] = ev

        MAX_ORDER = [i for k in range(TT // 2) for i in (TT - 1 - k, k)]

        def max_units(n):
            slot, two = n % RS, n % 2
            for i in MAX_ORDER:
                for j in range(G):
                    for piece in range(i // KQ + 1):
                        u = count["maxs"] % NM
                        count["maxs"] += 1
                        k0 = piece * QC
                        width = min(QC, (i + 1) * P - k0)
                        pe.wait(rows_ready[n], last("max_taken", u))
                        ev = pe.do(lambda e, u=u, i=i, j=j, k0=k0, width=width: e.matmul(
                            ps_m[:, u, 0:width], qr_sb[0:KR, slot, j, i * P:(i + 1) * P],
                            kr_sb[0:KR, slot, j, k0:k0 + width], start=True, stop=True), sig=pe_maxs)
                        m0 = QC - width if k0 + width == (i + 1) * P else 0
                        done["max_taken", u] = dve.do(lambda e, u=u, i=i, j=j, piece=piece, width=width, m0=m0, diag=(k0 + width == (i + 1) * P): e.tensor_tensor_reduce(
                            ps_m[:, u, 0:width], ps_m[:, u, 0:width],
                            mask_sb[:, 1, m0:QC] if diag else mask_sb[:, 0, 0:width], 1.0, -3e38,
                            ALU.add, ALU.max, mx_sb[:, two, piece, j * TT + i:j * TT + i + 1]),
                            after=[ev, last("max_parts", two)], sig=dve_max)
                        yield
            late = [mx_sb[:, two, piece, :].rearrange("p (j i) -> p j i", i=TT)[:, :, KQ:TT] for piece in range(2)]
            e1 = dve.do(lambda e: e.tensor_tensor(late[0], late[0], late[1], ALU.max), after=[dve_max.now()], sig=dve_max)
            hi, mid, lo = (mp_sb[:, two, i, :] for i in range(NP))
            e1 = dve.do(lambda e: e.tensor_scalar(hi, mx_sb[:, two, 0, :], -1.0, None, ALU.mult),
                        after=[e1, last("max_transposed", two)], sig=dve_max)
            e1 = dve.do(lambda e: e.scalar_tensor_tensor(out=mres_sb[:, two, :], in0=mx_sb[:, two, 0, :], scalar=-1.0,
                                                         in1=hi, op0=ALU.mult, op1=ALU.subtract), after=[e1], sig=dve_max)
            done["max_parts", two] = e1
            e1 = dve.do(lambda e: e.tensor_copy(mid, mres_sb[:, two, :]), after=[e1], sig=dve_max)
            ev_mp = dve.do(lambda e: e.tensor_tensor(lo, mres_sb[:, two, :], mid, ALU.subtract), after=[e1], sig=dve_max)
            yield
            nrow = NP * G * TT
            d = next_bank()
            mt_ps = ps_d[:, d, 0:P // 2].bitcast(BF16)
            ev = pe.do(lambda e: e.transpose(mt_ps[0:nrow, :], mp_sb[:, two, :, :].rearrange("p i n -> p (i n)"),
                                             idb_sb[:, :]), after=[ev_mp, last("dense_out", d)], sig=pe_dense)
            done["max_transposed", two] = ev
            e2 = act.do(lambda e: e.activation(mt_sb[0:nrow, two, :], mt_ps[0:nrow, :], ACT.Copy),
                        after=[ev, last("max_rows", two)], sig=act_dense)
            done["dense_out", d] = e2
            mrows_ready[n] = sp.do(lambda e: e.dma_start(
                qr_sb[KR:KR + NP, slot, :, :].rearrange("o j (i q) -> o (j i) q", q=P), mt_sb[0:nrow, two, :]),
                after=[e2], sig=mrows_in[slot], by=16)
            done["max_rows", two] = mrows_ready[n]
            yield

        MAX_STEPS = G * sum(i // KQ + 1 for i in range(TT)) + 2

        NORM_WAIT = 3

        def normalise(b, g, qc, ev_pv):
            k = count["y"] % 2
            count["y"] += 1
            e1 = act.do(lambda e: e.activation(yt_sb[:, k, :], ps_y[:, :], ACT.Copy),
                        after=[ev_pv, last("normalised", k)], sig=act_dense)
            done["y_out",] = e1
            spread = sp.do(lambda e: e.dma_start(den_sb[:, k, :], yt_sb[HS:HS + 32 * (G - 1) + 1:32, k, :]),
                           after=[e1, last("gathered_back", k)], sig=den_out[k], by=16)

            def later():
                for _ in range(NORM_WAIT):
                    yield
                e2 = dve.do(lambda e: e.reciprocal(den_sb[:, k, :], den_sb[:, k, :]), after=[spread], sig=dve_dense)
                back = sp.do(lambda e: e.dma_start(rden_sb[0:32 * (G - 1) + 1:32, :], den_sb[:, k, :]),
                             after=[e2, last("normalised_any")], sig=den_in[k], by=16)
                done["gathered_back", k] = back
                for _ in range(NORM_WAIT):
                    yield
                e3 = dve.do(lambda e: e.stream_shuffle(rden_sb[:, :], rden_sb[:, :], [0] * 32), after=[back],
                            sig=dve_dense)
                yield
                e4 = pool.do(lambda e: e.tensor_tensor(yn_sb[:, g, qc * QC:(qc + 1) * QC], yt_sb[:, k, :],
                                                       rden_sb[:, :], ALU.mult), after=[e3, last("projected")],
                             sig=pool_dense)
                done["normalised", k] = done["normalised_any",] = e4
                y_ready[b] = [e4]
            return later()

        def pv(tick):
            b, g, qc, kb, width, buf, ready = tick
            last_kb = KQ * (qc + 1) - 1
            pe.wait(ready, v_ready[b])
            if kb == 0:
                pe.wait(last("y_out"))
            for j in range(G):
                col = (G * g + j) * VW
                ev = pe.do(lambda e, j=j, col=col: e.matmul(
                    ps_y[32 * j:32 * j + 32, QC - width:QC], v_sb[:, b % 2, kb, col:col + 32],
                    pt_sb[:, buf, j, 0:width], start=(kb == 0), stop=(kb == last_kb)),
                    sig=pe_pv if j == G - 1 else None)
            done["pt_read", buf] = done["pv", b % 2] = ev
            if kb == last_kb:
                return normalise(b, g, qc, ev)
            return None

        def run(gen, n=None):
            while n is None or n > 0:
                if gen is None or next(gen, "end") == "end":
                    return
                if n is not None:
                    n -= 1

        def attention_tick(n, qc, kb, before, fill):
            b, g = divmod(n, NG)
            slot = n % RS
            buf = count["tick"] % 2
            count["tick"] += 1
            skip = max(0, kb - KQ * qc) * P
            width = QC - skip
            q0 = qc * QC + skip
            later = None
            for j in range(G):
                u = count["score"] % NS
                count["score"] += 1
                ev = pe.do(lambda e, j=j, u=u: e.matmul(
                    ps_s[:, u, 0:width], kr_sb[0:KR + NP, slot, j, kb * P:(kb + 1) * P],
                    qr_sb[0:KR + NP, slot, j, q0:q0 + width], start=True, stop=True),
                    after=[rows_ready[n], mrows_ready[n], last("exp", u)], sig=pe_score)
                e2 = act.do(lambda e, j=j, u=u: e.activation(pt_sb[:, buf, j, 0:width], ps_s[:, u, 0:width],
                                                             ACT.Exp, scale=SCALE),
                            after=[ev, last("pt_read", buf)], sig=act_exp)
                done["exp", u] = e2
                if j == 2 and before is not None:
                    later = pv(before)
                fill(j)
            done["scores", slot] = ev
            ready = e2
            if kb >= KQ * qc:
                diag = pt_sb[:, buf, :, 0:P]
                ready = pool.do(lambda e: e.affine_select(out=diag, in_=diag, compare_op=ALU.is_ge, fill=0.0, base=0,
                                                          pattern=[[0, G], [1, P]], channel_multiplier=-1),
                                after=[e2], sig=pool_mask)
            return (b, g, qc, kb, width, buf, ready), later

        def due(now, start, stop, steps):
            return max(0, min(steps, -(-steps * (now + 1 - start) // (stop - start))))

        run(first_ffn(0, alone=True))
        run(qkv(0, alone=True))
        run(gather_rows(0))
        run(gather_rows(1))
        run(max_units(0))

        n_groups = nb * NG
        ticks = [(qc, kb) for qc in range(NQC) for kb in range(KQ * (qc + 1))]
        NTK = len(ticks)
        GATHER_AT = 6
        before, later, gather = None, None, None
        for b in range(nb):
            streams = []
            if b > 0:
                streams.append([projection(b - 1), NCH, 3, 7, 0])
                streams.append([second_ffn(b - 1), NCH * FFN_STEPS, 7, NG * NTK - 1, 0])
            if b + 1 < nb:
                streams.append([first_ffn(b + 1), NCH * FFN_STEPS, 0, NTK + GATHER_AT - 3, 0])
                streams.append([qkv(b + 1), NCH * QKV_STEPS, NTK + GATHER_AT, 2 * NTK + GATHER_AT, 0])
            for g in range(NG):
                n = b * NG + g
                maxima = [max_units(n + 1), MAX_STEPS, 0] if n + 1 < n_groups else None
                for k, (qc, kb) in enumerate(ticks):
                    at = g * NTK + k
                    if k == GATHER_AT and n + 2 < n_groups:
                        gather = gather_rows(n + 2)

                    def fill(p, at=at, k=k):
                        run(later, 1)
                        run(gather, 1)
                        if maxima is not None:
                            goal = due(k * G + p, 0, (NTK - 1) * G, MAX_STEPS)
                            run(maxima[0], goal - maxima[2])
                            maxima[2] = goal
                        for st in streams:
                            goal = due(at * G + p, st[2] * G, st[3] * G, st[1])
                            run(st[0], goal - st[4])
                            st[4] = goal

                    before, nl = attention_tick(n, qc, kb, before, fill)
                    if nl is not None:
                        run(later)
                        later = nl
                if maxima is not None:
                    run(maxima[0])
            for st in streams:
                run(st[0])
        run(later)
        run(pv(before))
        run(projection(nb - 1))
        run(second_ffn(nb - 1, alone=True))
        for r in range(XR):
            for c in range(NCH):
                sp.wait(x_out[r][c].now())

        block = ctx.enter_context(nc.Block())

        @block.tensor
        def _(eng):
            pe.play(eng)

        @block.scalar
        def _(eng):
            act.play(eng)

        @block.vector
        def _(eng):
            dve.play(eng)

        @block.gpsimd
        def _(eng):
            pool.play(eng)

        @block.sync
        def _(eng):
            sp.play(eng)


def rope_tables():
    pos = np.arange(T, dtype=np.float32)[:, None]
    i = np.arange(1, HS // 2 + 1, dtype=np.float32)[None]
    theta = (np.float32(1.0) / np.float32(10000.0) ** (np.float32(2.0) * (i - np.float32(1.0)) / np.float32(HS))).astype(np.float32)
    ang = (pos * theta).astype(np.float32)
    cos, sin = np.cos(ang).T, np.sin(ang).T
    signed = np.stack([-sin, sin])
    cos = np.broadcast_to(cos[None, None, :, None, :], (2, 2, HS // 2, G, T))
    signed = np.broadcast_to(signed[None, :, :, None, :], (2, 2, HS // 2, G, T))
    return (np.ascontiguousarray(cos.reshape(P, T), dtype=np.float32),
            np.ascontiguousarray(signed.reshape(P, T), dtype=np.float32))


def kernel(L0_attn_x, L0_attn_W_qkv, L0_attn_b_qkv, L0_attn_W_proj, L0_attn_b_proj, L0_ffn_W_r, L0_ffn_W_k,
           L0_ffn_W_v, L0_ffn_mu_r, L0_ffn_mu_k):
    import concourse.bacc as bacc
    from concourse.bass_utils import run_bass_kernel_spmd

    x = np.ascontiguousarray(L0_attn_x)
    w = np.asarray(L0_attn_W_qkv).reshape(C, 2, 2, G, 3, HS // 2, 2)
    bq = np.asarray(L0_attn_b_qkv).reshape(2, 2, G, 3, HS // 2, 2)
    w_qk = w[:, :, :, :, 0:2].transpose(0, 4, 1, 2, 6, 5, 3).reshape(C, 2 * C)
    b_qk = bq[:, :, :, 0:2].transpose(3, 0, 1, 5, 4, 2).reshape(4, P).T
    w_v = np.asarray(L0_attn_W_qkv).reshape(C, H, 3, HS)[:, :, 2].reshape(C, C)
    b_v = np.asarray(L0_attn_b_qkv).reshape(H, 3, HS)[:, 2].reshape(1, C)
    rope_c, rope_s = rope_tables()
    arrays = {
        "x": x,
        "w_r": np.asarray(L0_ffn_W_r).T, "w_k": np.asarray(L0_ffn_W_k).T, "w_v": np.asarray(L0_ffn_W_v).T,
        "mu_r": np.asarray(L0_ffn_mu_r).reshape(CC, P).T, "mu_k": np.asarray(L0_ffn_mu_k).reshape(CC, P).T,
        "w_qk": w_qk, "b_qk": b_qk, "w_vv": w_v, "b_v": b_v,
        "w_p": np.asarray(L0_attn_W_proj), "b_p": np.asarray(L0_attn_b_proj).reshape(1, C),
        "rope_c": rope_c, "rope_s": rope_s,
    }
    arrays = {n: np.ascontiguousarray(a) for n, a in arrays.items()}
    nc = bacc.Bacc("TRN2", target_bir_lowering=False, num_devices=1)
    aps = {n: nc.dram_tensor(n, a.shape, mybir.dt.from_np(a.dtype), kind="ExternalInput").ap() for n, a in arrays.items()}
    out = nc.dram_tensor("out", x.shape, mybir.dt.from_np(x.dtype), kind="ExternalOutput").ap()
    macaron(nc, out=out, nb=x.shape[0], **aps)
    r = run_bass_kernel_spmd(nc, [arrays], core_ids=[0])
    return r.results[0]["out"]
```

```python
from contextlib import ExitStack

import numpy as np

import concourse.bass as bass
import concourse.mybir as mybir

F32 = mybir.dt.float32
BF16 = mybir.dt.bfloat16
ALU = mybir.AluOpType
ACT = mybir.ActivationFunctionType

P = 128
B, T, C = 16, 1024, 256
H, HS = 16, 16
EPS = 1e-5
CC = C // P
TT = T // P
CH = 256
CT = CH // P
NCH = T // CH
G = 4
NG = H // G
QC = 512
NQC = T // QC
KQ = QC // P
TERMS_Q = (0, 0, 0, 1, 1, 2)
TERMS_K = (0, 1, 2, 0, 1, 0)
NT = len(TERMS_Q)
KR = NT * HS
NP = 3
VW = HS + 1
VPAD = 32 - VW
NEG = -1e30
SCALE = HS ** -0.5


class Event:

    def __init__(self, sem, value, time=0.0):
        self.sem, self.value, self.time = sem, value, time


class Counter:

    def __init__(self, sem):
        self.sem, self.value, self.time = sem, 0, 0.0

    def bump(self, by, time):
        self.value += by
        self.time = time
        return Event(self, self.value, time)

    def now(self):
        return Event(self, self.value, self.time)


class Queue:

    def __init__(self, fixed, per, hop):
        self.ops, self.reached = [], {}
        self.fixed, self.per, self.hop, self.time = fixed, per, hop, 0.0

    def wait(self, *events):
        for e in events:
            if e is not None:
                self.time = max(self.time, e.time)
                if self.reached.get(e.sem, 0) < e.value:
                    self.reached[e.sem] = e.value
                    self.ops.append(lambda eng, s=e.sem.sem, v=e.value: eng.wait_ge(s, v))

    def do(self, make, after=(), sig=None, by=1, size=512):
        self.wait(*after)
        self.time += self.fixed + self.per * size
        if sig is None:
            self.ops.append(make)
            return None
        self.ops.append(lambda eng, s=sig.sem: make(eng).then_inc(s, by))
        return sig.bump(by, self.time + self.hop)

    def play(self, eng):
        for op in self.ops:
            op(eng)


class Chunk:
    running = None

    def __init__(self, steps, lag=0):
        self.steps, self.lag, self.need, self.count, self.over = steps, lag, 0.0, 0, False

    def advance(self):
        outer, Chunk.running = Chunk.running, self
        try:
            event = next(self.steps)
            self.need = event.time if event is not None else 0.0
            self.count += 1
        except StopIteration:
            self.over = True
        Chunk.running = outer


class Work:

    def __init__(self, chunks, lag=0, start=0, stop=0, steps=0):
        self.chunks = [c if isinstance(c, Chunk) else Chunk(c, lag) for c in chunks]
        self.open = len(chunks)
        self.start, self.stop, self.steps = start, stop, steps

    @property
    def done(self):
        return sum(c.count for c in self.chunks)

    def candidates(self):
        ahead = None
        for c in self.chunks[:self.open]:
            if ahead is not None and not ahead.over and ahead.count - c.count < c.lag:
                return
            if not c.over:
                yield c
            ahead = c

    def step(self, now=None):
        while True:
            c = min(self.candidates(), key=lambda c: c.need, default=None)
            if c is None or now is not None and c.need > now:
                return False
            c.advance()
            if not c.over:
                return True

    def need(self):
        return min([c.need for c in self.candidates()], default=0.0)

    def finish(self):
        while self.step():
            pass

    def due(self, at):
        return max(0, min(self.steps, -(-self.steps * (at + 1 - self.start) // (self.stop - self.start))))


def macaron(nc, x, w_r, w_k, w_v, mu_r, mu_k, w_qk, b_qk, w_vv, b_v, w_p, b_p, rope_c, rope_s, out, nb=B):
    ctx = ExitStack()
    with ctx:
        def sb(name, shape, dt=F32):
            return ctx.enter_context(nc.sbuf_tensor(name, shape, dt))

        def counter(name):
            return Counter(ctx.enter_context(nc.semaphore(name)))

        NS, NM, ND = 2, 3, 2
        XR = 3
        RS = 3
        x_sb = sb("x_sb", [P, XR, TT, C])
        xt_sb = sb("xt_sb", [P, 2, CT, C])
        xn_sb = sb("xn_sb", [P, 2, CC, CH + 1])
        dif_sb = sb("dif_sb", [P, 2, CC, CH])
        carry_sb = sb("carry_sb", [P, 2, CC, 1])
        ka_sb = sb("ka_sb", [P, 2, CC, CH])
        st_sb = sb("st_sb", [P, 2, CT, 6])
        mv_sb = sb("mv_sb", [P, 2, CT, 2])
        rs_sb = sb("rs_sb", [P, 2, CT])
        mhalf_sb = sb("mhalf_sb", [P, CT])
        qb_sb = sb("qb_sb", [P, 2, 2, CH])
        sw_sb = sb("sw_sb", [P, 2, 2, CH])
        part_sb = sb("part_sb", [P, NP, 4, T], BF16)
        v_sb = sb("v_sb", [P, 2, TT, H * VW + VPAD])
        qr_sb = sb("qr_sb", [P, RS, G, T], BF16)
        kr_sb = sb("kr_sb", [P, RS, G, T], BF16)
        pt_sb = sb("pt_sb", [P, 2, G, QC])
        yt_sb = sb("yt_sb", [P, 2, QC])
        den_sb = sb("den_sb", [P, 2, G * QC // P])
        rden_sb = sb("rden_sb", [P, QC])
        yn_sb = sb("yn_sb", [P, NG, T])
        mx_sb = sb("mx_sb", [P, 2, 2, G * TT])
        mres_sb = sb("mres_sb", [P, 2, G * TT])
        mp_sb = sb("mp_sb", [P, 2, NP, G * TT], BF16)
        mt_sb = sb("mt_sb", [P, 2, P], BF16)
        wr_sb = sb("wr_sb", [P, CC, C])
        wk_sb = sb("wk_sb", [P, CC, C])
        wv_sb = sb("wv_sb", [P, CC, C])
        wqk_sb = sb("wqk_sb", [P, CC, 2 * C])
        wvv_sb = sb("wvv_sb", [P, CC, C])
        wp_sb = sb("wp_sb", [P, NG, C])
        mur_sb = sb("mur_sb", [P, CC])
        muk_sb = sb("muk_sb", [P, CC])
        bqk_sb = sb("bqk_sb", [P, 4])
        bv_sb = sb("bv_sb", [P, C])
        cos_sb = sb("cos_sb", [P, T])
        sin_sb = sb("sin_sb", [P, T])
        mask_sb = sb("mask_sb", [P, 2, QC], BF16)
        id_sb = sb("id_sb", [P, P])
        idb_sb = sb("idb_sb", [P, P], BF16)

        ps_s = ctx.enter_context(nc.psum_tensor("ps_s", [P, NS, QC], F32))
        ps_m = ctx.enter_context(nc.psum_tensor("ps_m", [P, NM, QC], F32))
        ps_y = ctx.enter_context(nc.psum_tensor("ps_y", [P, QC], F32))
        ps_d = ctx.enter_context(nc.psum_tensor("ps_d", [P, ND, QC], F32))

        consts_ffn = counter("consts_ffn")
        consts = counter("consts")
        x_in = [[counter(f"x_in{r}_{c}") for c in range(NCH)] for r in range(XR)]
        x_out = [[counter(f"x_out{r}_{c}") for c in range(NCH)] for r in range(XR)]
        swapped = [counter("swapped_q"), counter("swapped_k")]
        rows_in = [counter(f"rows_in{r}") for r in range(RS)]
        mrows_in = [counter(f"mrows_in{r}") for r in range(RS)]
        den_out = [counter("den_out0"), counter("den_out1")]
        den_in = [counter("den_in0"), counter("den_in1")]
        pe_score = counter("pe_score")
        pe_maxs = counter("pe_maxs")
        pe_pv = counter("pe_pv")
        pe_dense = counter("pe_dense")
        act_exp = counter("act_exp")
        act_dense = counter("act_dense")
        dve_max = counter("dve_max")
        dve_dense = counter("dve_dense")
        pool_mask = counter("pool_mask")
        pool_dense = counter("pool_dense")
        setup = counter("setup")
        setup_dve = counter("setup_dve")

        pe, act, dve, pool = Queue(0.0, 1 / 2400, 0.2), Queue(0.05, 1 / 1200, 0.1), Queue(0.06, 1 / 960, 0.1), Queue(0.15, 1 / 480, 0.1)
        sp = Queue(0.65, 0.0, 1.6)

        def chunked(w):
            return w.rearrange("(c p) n -> p c n", p=P)

        ev_zero = pool.do(lambda e: e.memset(wp_sb[:, :, :], 0.0), sig=setup)
        ffn_loads = [
            (wr_sb[:, :, :], chunked(w_r)), (wk_sb[:, :, :], chunked(w_k)), (wv_sb[:, :, :], chunked(w_v)),
            (mur_sb[:, :], mu_r), (muk_sb[:, :], mu_k),
        ]
        const_loads = [
            (wqk_sb[:, :, :], chunked(w_qk)), (wvv_sb[:, :, :], chunked(w_vv)),
            (bqk_sb[:, :], b_qk),
            (bv_sb[:, :], b_v.broadcast_to([P, C])), (cos_sb[:, :], rope_c), (sin_sb[:, :], rope_s),
        ]

        def load_x(b, c):
            r = b % XR
            src = x[b].rearrange("(t p) c -> p t c", p=P)[:, c * CT:(c + 1) * CT, :]
            return sp.do(lambda e: e.dma_start(x_sb[:, r, c * CT:(c + 1) * CT, :], src),
                         after=[x_out[r][c].now()], sig=x_in[r][c], by=16)

        x_ready = {}
        for c in range(NCH):
            x_ready[0, c] = load_x(0, c)
            if c == 0:
                for dst, src in ffn_loads:
                    sp.do(lambda e, d=dst, s=src: e.dma_start(d, s), sig=consts_ffn, by=16)
        ev_ffn = consts_ffn.now()
        for dst, src in const_loads:
            sp.do(lambda e, d=dst, s=src: e.dma_start(d, s), sig=consts, by=16)
        sp.wait(ev_zero)
        for g in range(NG):
            for j in range(G):
                h = G * g + j
                sp.do(lambda e, g=g, j=j, h=h: e.dma_start(wp_sb[32 * j:32 * j + HS, g, :], w_p[h * HS:(h + 1) * HS, :]),
                      sig=consts, by=16)
        sp.do(lambda e: e.dma_start(wp_sb[HS:HS + 1, 0, :], b_p), sig=consts, by=16)
        ev_const = consts.now()
        for b in range(1, min(nb, XR)):
            for c in range(NCH):
                x_ready[b, c] = load_x(b, c)

        pool.do(lambda e: e.memset(id_sb[:, :], 0.0), sig=setup)
        pool.do(lambda e: e.memset(idb_sb[:, :], 0.0), sig=setup)
        ev_mz = pool.do(lambda e: e.memset(mask_sb[:, :, :], 0.0), sig=setup)
        pool.wait(ev_mz)
        for t in (id_sb, idb_sb):
            pool.do(lambda e, t=t: e.affine_select(out=t[:, :], in_=t[:, :], compare_op=ALU.not_equal, fill=1.0,
                                                   base=0, pattern=[[-1, P]], channel_multiplier=1), sig=setup)
        pool.do(lambda e: e.affine_select(out=mask_sb[:, 1, QC - P:QC], in_=mask_sb[:, 1, QC - P:QC], compare_op=ALU.is_ge,
                                          fill=NEG, base=0, pattern=[[-1, P]], channel_multiplier=1), sig=setup)
        dve.do(lambda e: e.memset(rden_sb[:, :], 1.0), sig=setup_dve)
        pool.do(lambda e: e.memset(mhalf_sb[:, :], -0.5), sig=setup)
        heads = v_sb[:, :, :, 0:H * VW].rearrange("p b t (h w) -> p (b t) h w", w=VW)
        pool.do(lambda e: e.memset(heads[:, :, :, HS:VW], 1.0), sig=setup)
        ev_setup = pool.do(lambda e: e.memset(v_sb[:, :, :, H * VW:], 1.0), sig=setup)
        ev_wv = dve.do(lambda e: e.tensor_scalar(wv_sb[:, :, :], wv_sb[:, :, :], 0.25, None, ALU.mult),
                       after=[ev_ffn], sig=setup_dve)
        for q in (pe, act, dve, pool):
            q.wait(ev_ffn, ev_setup)
        pe.wait(ev_wv)

        count = {"score": 0, "maxs": 0, "tick": 0, "y": 0, "dense": 0}
        done = {}

        def last(*step):
            return done.get(step)

        def layernorm(b, c, s):
            r = b % XR
            for t in range(CT):
                ev = dve.do(lambda e, t=t: e.bn_stats(st_sb[:, s, t, :], x_sb[:, r, c * CT + t, :]),
                            after=[x_ready[b, c]], sig=dve_dense, size=256)
            for t in range(CT):
                ev_mv = dve.do(lambda e, t=t: e.bn_aggr(mv_sb[:, s, t, :], st_sb[:, s, t, :]),
                               after=[ev, last("rstd", s)], sig=dve_dense, size=16)
            yield ev_mv
            ev = pool.do(lambda e: e.tensor_scalar(rs_sb[:, s, :], mv_sb[:, s, :, 1], EPS, None, ALU.add),
                         after=[ev_mv, last("normed", s)], sig=pool_dense, size=16)
            done["rstd", s] = ev
            ev = pool.do(lambda e: e.tensor_tensor(rs_sb[:, s, :], rs_sb[:, s, :], mhalf_sb[:, :], ALU.pow),
                         after=[ev], sig=pool_dense, size=240)
            yield ev
            for t in range(CT):
                ev_xt = dve.do(lambda e, t=t: e.tensor_scalar(
                    xt_sb[:, s, t, :], x_sb[:, r, c * CT + t, :], mv_sb[:, s, t, 0:1], rs_sb[:, s, t:t + 1],
                    ALU.subtract, ALU.mult), after=[ev, last("transposed", s), last("x_added", s)], sig=dve_dense, size=256)
            done["normed", s] = ev_xt
            yield ev_xt
            return ev_xt

        READ_SLACK = 0.25
        held = {}

        def next_bank():
            count["dense"] += 1
            if count["dense"] % ND in held and len(held) < ND:
                count["dense"] += 1
            d = count["dense"] % ND
            if d in held:
                held[d].advance()
                assert d not in held
            return d

        def hold(d, ev):
            held[d] = Chunk.running
            return ev

        def read_ready():
            for chunk in list(held.values()):
                if chunk.need <= pe.time + READ_SLACK:
                    chunk.advance()

        def read(d, ev):
            done["dense_out", d] = ev
            held.pop(d, None)

        def transposed(s, ev_xt, ev_carry=None):
            d = next_bank()
            pe.wait(ev_xt, last("dense_out", d))
            for cc in range(CC):
                for t in range(CT):
                    final = (cc, t) == (CC - 1, CT - 1)
                    ev = pe.do(lambda e, d=d, cc=cc, t=t: e.transpose(
                        ps_d[:, d, cc * CH + t * P:cc * CH + (t + 1) * P], xt_sb[:, s, t, cc * P:(cc + 1) * P],
                        id_sb[:, :]), sig=pe_dense if final else None, size=P)
            done["transposed", s] = ev
            yield hold(d, ev)
            e2 = act.do(lambda e, d=d: e.activation(xn_sb[:, s, :, 1:CH + 1],
                                               by_half(ps_d[:, d, :]), ACT.Copy),
                        after=[ev, ev_carry, last("mixed", s), last("v_made", s)],
                        sig=act_dense)
            read(d, e2)
            return e2

        def product(parts, after):
            d = next_bank()
            pe.wait(*after, last("dense_out", d))
            for n, (cols, pairs) in enumerate(parts):
                for k, (l, r) in enumerate(pairs):
                    final = n == len(parts) - 1 and k == len(pairs) - 1
                    ev = pe.do(lambda e, d=d, cols=cols, l=l, r=r, k=k, m=len(pairs): e.matmul(
                        ps_d[:, d, cols], l, r, start=(k == 0), stop=(k == m - 1)), sig=pe_dense if final else None, size=4 * CH)
            return ev, d

        def halves(n):
            return slice(n * CH, (n + 1) * CH)

        def by_half(ap):
            return ap.rearrange("p (t n) -> p t n", t=CT)

        v_ready, parts_ready, y_ready, projected = {}, {}, {}, {}

        def ffn_chunk(b, c, s, finish=None):
            r = b % XR
            ev_xt = yield from layernorm(b, c, s)
            first = slice(0, 1)
            k = 0 if finish is None else 1
            if c == 0:
                ev_carry = pool.do(lambda e: e.memset(xn_sb[:, s, :, first], 0.0), after=[last("mixed", s)], sig=pool_dense)
            else:
                ev_carry = pool.do(lambda e: e.tensor_copy(xn_sb[:, s, :, first], carry_sb[:, k, :, :]),
                                   after=[last("carry_saved", k), last("mixed", s)], sig=pool_dense)
            ev_xn = yield from transposed(s, ev_xt, ev_carry)
            yield ev_xn
            done["carry_saved", k] = ev_saved = pool.do(
                lambda e: e.tensor_copy(carry_sb[:, k, :, :], xn_sb[:, s, :, CH:CH + 1]),
                after=[ev_xn, ev_carry], sig=pool_dense)
            cur, prev = xn_sb[:, s, :, 1:CH + 1], xn_sb[:, s, :, 0:CH]
            ev_d = pool.do(lambda e: e.tensor_tensor(dif_sb[:, s, :, :], cur, prev, ALU.subtract),
                           after=[ev_xn, ev_saved, last("r_made", s)], sig=pool_dense)
            yield ev_d
            for cc in range(CC):
                ev_xk = dve.do(lambda e, cc=cc: e.scalar_tensor_tensor(
                    out=ka_sb[:, s, cc, :], in0=dif_sb[:, s, cc, :], scalar=muk_sb[:, cc:cc + 1],
                    in1=xn_sb[:, s, cc, 0:CH], op0=ALU.mult, op1=ALU.add), after=[ev_d, last("kv_made", s)], sig=dve_dense, size=320)
            for cc in range(CC):
                ev_xr = dve.do(lambda e, cc=cc: e.scalar_tensor_tensor(
                    out=dif_sb[:, s, cc, :], in0=dif_sb[:, s, cc, :], scalar=mur_sb[:, cc:cc + 1],
                    in1=xn_sb[:, s, cc, 0:CH], op0=ALU.mult, op1=ALU.add), after=[ev_xk], sig=dve_dense, size=320)
            done["mixed", s] = ev_xr
            yield ev_xk
            ev, d = product([(halves(m), [(wk_sb[:, cc, m * P:(m + 1) * P], ka_sb[:, s, cc, :]) for cc in range(CC)])
                          for m in range(CC)], [ev_xk])
            yield hold(d, ev)
            ev_relu = act.do(lambda e, d=d: e.activation(ka_sb[:, s, :, :], by_half(ps_d[:, d, :]), ACT.Relu),
                             after=[ev, last("kv_made", s)], sig=act_dense)
            read(d, ev_relu)
            yield ev_relu
            ev_ka = act.do(lambda e: e.activation(ka_sb[:, s, :, :], ka_sb[:, s, :, :], ACT.Square),
                           after=[ev_relu], sig=act_dense)
            ev, d = product([(halves(t), [(dif_sb[:, s, cc, t * P:(t + 1) * P], wr_sb[:, cc, :]) for cc in range(CC)])
                          for t in range(CT)], [ev_xr])
            done["r_made", s] = ev
            yield hold(d, ev)
            ev_th = act.do(lambda e, d=d: e.activation(xt_sb[:, s, :, :], by_half(ps_d[:, d, :]), ACT.Tanh, scale=0.5),
                           after=[ev, last("transposed", s)], sig=act_dense)
            read(d, ev_th)
            yield ev_ka
            ev, d = product([(halves(t), [(ka_sb[:, s, cc, t * P:(t + 1) * P], wv_sb[:, cc, :]) for cc in range(CC)])
                          for t in range(CT)], [ev_ka])
            done["kv_made", s] = ev
            yield hold(d, ev)
            ev_u = dve.do(lambda e, d=d: e.scalar_tensor_tensor(
                out=xt_sb[:, s, :, :], in0=xt_sb[:, s, :, :], scalar=1.0, in1=by_half(ps_d[:, d, :]),
                op0=ALU.add, op1=ALU.mult), after=[ev, ev_th], sig=dve_dense)
            read(d, ev_u)
            yield ev_u
            xc = x_sb[:, r, c * CT:(c + 1) * CT, :]
            x_ready[b, c] = pool.do(lambda e: e.tensor_tensor(xc, xc, xt_sb[:, s, :, :], ALU.add),
                                    after=[ev_u, x_ready[b, c]], sig=pool_dense)
            done["x_added", s] = x_ready[b, c]
            if finish is not None:
                finish(b, c)
            yield

        FFN_STEPS = 14

        def qkv_chunk(b, c, s):
            ev_xt = yield from layernorm(b, c, s)
            ev_xn = yield from transposed(s, ev_xt)
            yield ev_xn
            biased, turned = [], []
            for n in range(2):
                ev, d = product([(halves(m), [(wqk_sb[:, cc, (2 * n + m) * P:(2 * n + m + 1) * P],
                                            xn_sb[:, s, cc, 1:CH + 1]) for cc in range(CC)]) for m in range(2)], [ev_xn])
                yield hold(d, ev)
                for m in range(2):
                    eb = act.do(lambda e, d=d, m=m, n=n: e.activation(
                        qb_sb[:, n, m, :], ps_d[:, d, halves(m)], ACT.Identity, bias=bqk_sb[:, 2 * n + m:2 * n + m + 1]),
                        after=[ev, last("low_made", n)], sig=act_dense, size=256)
                read(d, eb)
                sp.wait(eb, last("turned", n))
                for q in range(4):
                    es = sp.do(lambda e, n=n, q=q: e.dma_start(
                        sw_sb[32 * q:32 * q + 32, n, :, :], qb_sb[32 * (q ^ 1):32 * (q ^ 1) + 32, n, :, :]),
                        sig=swapped[n], by=16)
                biased.append(eb)
                turned.append(es)
                yield
            ev, d = product([(halves(t), [(xn_sb[:, s, cc, 1 + t * P:1 + (t + 1) * P], wvv_sb[:, cc, :])
                                       for cc in range(CC)]) for t in range(CT)], [ev_xn])
            done["v_made", s] = ev
            yield hold(d, ev)
            for t in range(CT):
                dst = v_sb[:, b % 2, c * CT + t, 0:H * VW].rearrange("p (h w) -> p h w", w=VW)[:, :, 0:HS]
                v_ready[b] = dve.do(lambda e, d=d, t=t, dst=dst: e.tensor_tensor(
                    dst, ps_d[:, d, halves(t)].rearrange("p (h d) -> p h d", d=HS),
                    bv_sb[:, :].rearrange("p (h d) -> p h d", d=HS), ALU.add),
                    after=[ev, last("pv", b % 2)], sig=dve_dense, size=256)
            read(d, v_ready[b])
            yield turned[0]
            cols = slice(c * CH, (c + 1) * CH)
            cos = cos_sb[:, cols].rearrange("p (o n) -> p o n", o=1).broadcast_to([P, 2, CH])
            sin = sin_sb[:, cols].rearrange("p (o n) -> p o n", o=1).broadcast_to([P, 2, CH])
            q = [qb_sb[:, n, :, :] for n in range(2)]
            w = [sw_sb[:, n, :, :] for n in range(2)]
            part = [[part_sb[:, i, 2 * n:2 * n + 2, cols] for i in range(NP)] for n in range(2)]
            ev1, ev2, ev3, ev4, ev5, ev6 = [{} for _ in range(6)]
            newest = [None]

            def turn(n):
                ev1[n] = pool.do(lambda e: e.tensor_tensor(q[n], q[n], cos, ALU.mult), after=[biased[n], turned[n]],
                                 sig=pool_dense)
                ev2[n] = dve.do(lambda e: e.tensor_tensor(w[n], w[n], sin, ALU.mult), after=[turned[n]], sig=dve_dense)
                newest[0] = ev1[n]

            def add(n):
                ev3[n] = dve.do(lambda e: e.tensor_tensor(q[n], q[n], w[n], ALU.add), after=[ev1[n], ev2[n]],
                                sig=dve_dense)
                done["turned", n] = newest[0] = ev3[n]

            def high(n):
                ev4[n] = act.do(lambda e: e.activation(part[n][0], q[n], ACT.Copy),
                                after=[ev3[n], last("all_gathered")], sig=act_dense)
                newest[0] = ev4[n]

            def rest(n):
                ev5[n] = pool.do(lambda e: e.tensor_tensor(q[n], q[n], part[n][0], ALU.subtract), after=[ev4[n]],
                                 sig=pool_dense)
                newest[0] = ev5[n]

            def middle(n):
                ev6[n] = act.do(lambda e: e.activation(part[n][1], q[n], ACT.Copy), after=[ev5[n]], sig=act_dense)
                newest[0] = ev6[n]

            def low(n):
                ev = pool.do(lambda e: e.tensor_tensor(part[n][2], q[n], part[n][1], ALU.subtract),
                             after=[ev6[n], last("all_gathered")], sig=pool_dense)
                done["low_made", n] = ev
                parts_ready[b] = parts_ready.get(b, []) + [ev4[n], ev6[n], ev]

            todo = [turn, add, high, rest, middle, low]
            for step in range(len(todo) + 1):
                if step < len(todo):
                    todo[step](0)
                if step > 0:
                    todo[step - 1](1)
                yield newest[0]

        QKV_STEPS = 18

        def proj_chunk(b, c):
            r = b % XR
            ev, d = product([(halves(t), [(yn_sb[:, g, (c * CT + t) * P:(c * CT + t + 1) * P], wp_sb[:, g, :])
                                       for g in range(NG)]) for t in range(CT)], y_ready[b])
            done["projected",] = ev
            projected[b] = projected.get(b, 0) + 1
            yield hold(d, ev)
            xc = x_sb[:, r, c * CT:(c + 1) * CT, :]
            x_ready[b, c] = dve.do(lambda e, d=d: e.tensor_tensor(xc, xc, by_half(ps_d[:, d, :]), ALU.add),
                                   after=[ev, x_ready[b, c]], sig=dve_dense)
            read(d, x_ready[b, c])
            yield

        def store(b, c):
            r = b % XR
            dst = out[b].rearrange("(t p) c -> p t c", p=P)[:, c * CT:(c + 1) * CT, :]
            sp.do(lambda e: e.dma_start(dst, x_sb[:, r, c * CT:(c + 1) * CT, :]), after=[x_ready[b, c]],
                  sig=x_out[r][c], by=16)
            if b + XR < nb:
                x_ready[b + XR, c] = load_x(b + XR, c)

        def incoming(b, **when):
            return Work([Chunk(ffn_chunk(b, c, c % 2), FFN_STEPS // 2) for c in range(NCH)] +
                        [Chunk(qkv_chunk(b, c, c % 2), QKV_LAG if c else FFN_STEPS // 2) for c in range(NCH)],
                        steps=NCH * (FFN_STEPS + QKV_STEPS), **when)

        def first_chunks(b):
            def both(c):
                yield from ffn_chunk(b, c, c % 2)
                if c == 0:
                    for q in (pe, act, dve, pool):
                        q.wait(ev_const)
                yield from qkv_chunk(b, c, c % 2)
            return Work([both(c) for c in range(NCH)], (FFN_STEPS + QKV_STEPS) // 2)

        def second_ffn(b, **when):
            return Work([ffn_chunk(b, c, c % 2, store) for c in range(NCH)], FFN_STEPS // 2, steps=NCH * FFN_STEPS, **when)

        def last_chunks(b, **when):
            def both(c):
                yield from proj_chunk(b, c)
                yield from ffn_chunk(b, c, c % 2, store)
            steps = PROJ_STEPS + FFN_STEPS
            return Work([both(c) for c in range(NCH)], steps // 2, steps=NCH // 2 * steps, **when)

        PROJ_STEPS = 2
        QKV_LAG = 12

        def projection(b, **when):
            return Work([proj_chunk(b, c) for c in range(NCH)], 1, steps=PROJ_STEPS * NCH, **when)

        rows_ready, mrows_ready, ev_ones = {}, {}, {}

        def gather_rows(n):
            b, g = divmod(n, NG)
            slot, m, base = n % RS, g // 2, 64 * (g % 2)
            assert len(parts_ready[b]) == 6 * NCH
            sp.wait(*parts_ready[b], last("scores", slot))
            for dst, tile, terms in ((kr_sb, 2 + m, TERMS_K), (qr_sb, m, TERMS_Q)):
                for t, part in enumerate(terms):
                    ev = sp.do(lambda e, dst=dst, tile=tile, t=t, part=part: e.dma_start(
                        dst[t * HS:(t + 1) * HS, slot, :, :], part_sb[base:base + 64, part, tile, :]),
                        sig=rows_in[slot], by=16)
                    if t % 2:
                        yield
            rows_ready[n] = ev
            if g == NG - 1:
                done["all_gathered",] = ev

        MAX_ORDER = [i for k in range(TT // 2) for i in (TT - 1 - k, k)]

        def max_units(n):
            slot, two = n % RS, n % 2
            yield rows_ready[n]
            for i in MAX_ORDER:
                for j in range(G):
                    for piece in range(i // KQ + 1):
                        u = count["maxs"] % NM
                        count["maxs"] += 1
                        k0 = piece * QC
                        width = min(QC, (i + 1) * P - k0)
                        pe.wait(rows_ready[n], last("max_taken", u))
                        ev = pe.do(lambda e, u=u, i=i, j=j, k0=k0, width=width: e.matmul(
                            ps_m[:, u, 0:width], qr_sb[0:KR, slot, j, i * P:(i + 1) * P],
                            kr_sb[0:KR, slot, j, k0:k0 + width], start=True, stop=True), sig=pe_maxs, size=width)
                        m0 = QC - width if k0 + width == (i + 1) * P else 0
                        done["max_taken", u] = dve.do(lambda e, u=u, i=i, j=j, piece=piece, width=width, m0=m0, diag=(k0 + width == (i + 1) * P): e.tensor_tensor_reduce(
                            ps_m[:, u, 0:width], ps_m[:, u, 0:width],
                            mask_sb[:, 1, m0:QC] if diag else mask_sb[:, 0, 0:width], 1.0, -3e38,
                            ALU.add, ALU.max, mx_sb[:, two, piece, j * TT + i:j * TT + i + 1]),
                            after=[ev, last("max_parts", two)], sig=dve_max, size=width)
                        yield last("max_taken", count["maxs"] % NM)
            late = [mx_sb[:, two, piece, :].rearrange("p (j i) -> p j i", i=TT)[:, :, KQ:TT] for piece in range(2)]
            e1 = dve.do(lambda e: e.tensor_tensor(late[0], late[0], late[1], ALU.max), after=[dve_max.now()], sig=dve_max)
            hi, mid, lo = (mp_sb[:, two, i, :] for i in range(NP))
            e1 = dve.do(lambda e: e.tensor_scalar(hi, mx_sb[:, two, 0, :], -1.0, None, ALU.mult),
                        after=[e1, last("max_transposed", two)], sig=dve_max)
            e1 = dve.do(lambda e: e.scalar_tensor_tensor(out=mres_sb[:, two, :], in0=mx_sb[:, two, 0, :], scalar=-1.0,
                                                         in1=hi, op0=ALU.mult, op1=ALU.subtract), after=[e1], sig=dve_max)
            done["max_parts", two] = e1
            e1 = dve.do(lambda e: e.tensor_copy(mid, mres_sb[:, two, :]), after=[e1], sig=dve_max)
            ev_mp = dve.do(lambda e: e.tensor_tensor(lo, mres_sb[:, two, :], mid, ALU.subtract), after=[e1], sig=dve_max,
                           size=320)
            yield ev_mp
            nrow = NP * G * TT
            d = next_bank()
            mt_ps = ps_d[:, d, 0:P // 2].bitcast(BF16)
            ev = pe.do(lambda e: e.transpose(mt_ps[0:nrow, :], mp_sb[:, two, :, :].rearrange("p i n -> p (i n)"),
                                             idb_sb[:, :]), after=[ev_mp, last("dense_out", d)], sig=pe_dense)
            done["max_transposed", two] = ev
            e2 = act.do(lambda e: e.activation(mt_sb[0:nrow, two, :], mt_ps[0:nrow, :], ACT.Copy),
                        after=[ev, last("max_rows", two)], sig=act_dense)
            done["dense_out", d] = e2
            mrows_ready[n] = sp.do(lambda e: e.dma_start(
                qr_sb[KR:KR + NP, slot, :, :].rearrange("o j (i q) -> o (j i) q", q=P), mt_sb[0:nrow, two, :]),
                after=[e2], sig=mrows_in[slot], by=16)
            done["max_rows", two] = mrows_ready[n]
            yield

        MAX_STEPS = G * sum(i // KQ + 1 for i in range(TT)) + 3

        def normalise(b, g, qc, ev_pv):
            k = count["y"] % 2
            count["y"] += 1
            e1 = act.do(lambda e: e.activation(yt_sb[:, k, :], ps_y[:, :], ACT.Copy),
                        after=[ev_pv, last("normalised", k)], sig=act_dense)
            done["y_out",] = e1
            spread = sp.do(lambda e: e.dma_start(den_sb[:, k, :], yt_sb[HS:HS + 32 * (G - 1) + 1:32, k, :]),
                           after=[e1, last("gathered_back", k)], sig=den_out[k], by=16)

            def later():
                yield spread
                e2 = dve.do(lambda e: e.reciprocal(den_sb[:, k, :], den_sb[:, k, :]), after=[spread], sig=dve_dense, size=100)
                back = sp.do(lambda e: e.dma_start(rden_sb[0:32 * (G - 1) + 1:32, :], den_sb[:, k, :]),
                             after=[e2, last("normalised_any")], sig=den_in[k], by=16)
                done["gathered_back", k] = back
                yield back
                e3 = dve.do(lambda e: e.stream_shuffle(rden_sb[:, :], rden_sb[:, :], [0] * 32), after=[back],
                            sig=dve_dense)
                yield e3
                assert g or qc or not b or projected[b - 1] == NCH
                e4 = pool.do(lambda e: e.tensor_tensor(yn_sb[:, g, qc * QC:(qc + 1) * QC], yt_sb[:, k, :],
                                                       rden_sb[:, :], ALU.mult), after=[e3, last("projected")],
                             sig=pool_dense)
                done["normalised", k] = done["normalised_any",] = e4
                y_ready[b] = [e4]
            return Work([later()], 1)

        def pv(tick):
            b, g, qc, kb, width, buf, ready = tick
            last_kb = KQ * (qc + 1) - 1
            pe.wait(ready, v_ready[b])
            if kb == 0:
                pe.wait(last("y_out"))
            for j in range(G):
                col = (G * g + j) * VW
                ev = pe.do(lambda e, j=j, col=col: e.matmul(
                    ps_y[32 * j:32 * j + 32, QC - width:QC], v_sb[:, b % 2, kb, col:col + 32],
                    pt_sb[:, buf, j, 0:width], start=(kb == 0), stop=(kb == last_kb)),
                    sig=pe_pv if j == G - 1 else None, size=width)
            done["pt_read", buf] = done["pv", b % 2] = ev
            if kb == last_kb:
                return normalise(b, g, qc, ev)
            return None

        def attention_tick(n, qc, kb, before, fill):
            b, g = divmod(n, NG)
            slot = n % RS
            buf = count["tick"] % 2
            count["tick"] += 1
            skip = max(0, kb - KQ * qc) * P
            width = QC - skip
            q0 = qc * QC + skip
            later = None
            for j in range(G):
                u = count["score"] % NS
                count["score"] += 1
                ev = pe.do(lambda e, j=j, u=u: e.matmul(
                    ps_s[:, u, 0:width], kr_sb[0:KR + NP, slot, j, kb * P:(kb + 1) * P],
                    qr_sb[0:KR + NP, slot, j, q0:q0 + width], start=True, stop=True),
                    after=[rows_ready[n], mrows_ready[n], ev_ones[slot], last("exp", u)], sig=pe_score, size=width)
                e2 = act.do(lambda e, j=j, u=u: e.activation(pt_sb[:, buf, j, 0:width], ps_s[:, u, 0:width],
                                                             ACT.Exp, scale=SCALE),
                            after=[ev, last("pt_read", buf)], sig=act_exp, size=width)
                done["exp", u] = e2
                fill(j, last("exp", (u + 1) % NS))
                if before is not None and (j == PV_LAST or j >= PV_AT and before[-1].time <= pe.time + PV_SLACK):
                    if j == PV_LAST:
                        fill(j, before[-1])
                    later = pv(before)
                    before = None
            done["scores", slot] = ev
            ready = e2
            if kb >= KQ * qc:
                diag = pt_sb[:, buf, :, 0:P]
                ready = pool.do(lambda e: e.affine_select(out=diag, in_=diag, compare_op=ALU.is_ge, fill=0.0, base=0,
                                                          pattern=[[0, G], [1, P]], channel_multiplier=-1),
                                after=[e2], sig=pool_mask)
            return (b, g, qc, kb, width, buf, ready), later

        first_chunks(0).finish()
        pool.wait(pool_dense.now())
        for slot in range(RS):
            ev_ones[slot] = pool.do(lambda e, slot=slot: e.memset(kr_sb[KR:KR + NP, slot, :, :], 1.0), sig=setup)
            pool.wait(ev_ones[slot])
        for n in range(2):
            Work([gather_rows(n)], 1).finish()
        Work([max_units(0)], 1).finish()

        n_groups = nb * NG
        ticks = [(qc, kb) for qc in range(NQC) for kb in range(KQ * (qc + 1))]
        NTK = len(ticks)
        PV_AT, PV_LAST = 2, 3
        PV_SLACK = 0.0
        GATHER_AT = [4, 1, 7, 4]
        PROJ_START, PROJ_STOP = 4, KQ + 1
        QKV_START, IN_STOP = 14, 31
        assert NTK + GATHER_AT[1] < QKV_START and IN_STOP <= 2 * NTK + GATHER_AT[2]
        SLACK, EARLY = 0.0, 24
        NEAR, VERY_LATE = 1.0, 10
        LATE_MAX, LATE = 10, 5
        END_START = KQ + 3
        ending_start = ((NG - 1) * NTK + END_START) * G

        def maxima_of(m):
            return Work([max_units(m)], 1, ((m - 1) * NTK - MAX_AHEAD) * G, (m * NTK - MAX_MARGIN) * G, MAX_STEPS)

        MAX_AHEAD, MAX_MARGIN = 2, 2
        maxima = {1: maxima_of(1)}
        before, later, gather = None, None, None
        for b in range(nb):
            streams = []
            if b > 0:
                streams.append(projection(b - 1, start=PROJ_START * G, stop=PROJ_STOP * G))
                between = (IN_STOP, NG * NTK - 1) if b + 1 < nb else (PROJ_STOP + 1, (NG - 1) * NTK)
                streams.append(second_ffn(b - 1, start=between[0] * G, stop=between[1] * G))
            if b + 1 == nb:
                ending = last_chunks(b, start=ending_start, stop=NG * NTK * G)
                ending.open = NCH // 2
                streams.append(ending)
            if b + 1 < nb:
                streams.append(incoming(b + 1, start=0, stop=(IN_STOP - 1) * G))
                streams[-1].open = NCH
            for g in range(NG):
                n = b * NG + g
                for k, (qc, kb) in enumerate(ticks):
                    at = (g * NTK + k) * G
                    if k == NTK - MAX_AHEAD and n + 2 < n_groups:
                        gather.finish()
                        maxima[n + 2] = maxima_of(n + 2)
                    if at == PROJ_STOP * G and b > 0:
                        if later is not None:
                            later.finish()
                        streams[0].finish()
                    if at == QKV_START * G and b + 1 < nb:
                        gather.finish()
                        streams[-1].open = 2 * NCH
                    if at == IN_STOP * G and b + 1 < nb:
                        streams[-1].finish()
                    if at == ending_start and b + 1 == nb:
                        later.finish()
                        for st in streams[:-1]:
                            st.finish()
                    if k == GATHER_AT[g] and n + 2 < n_groups:
                        gather = Work([gather_rows(n + 2)], 1)

                    def fill(p, bank, at=at, n=n, k=k):
                        if later is not None:
                            later.step(pe.time)
                        if gather is not None:
                            gather.step()
                        now = [(m, (n * NTK + k) * G + p) for m in maxima.values()]
                        now += [(st, at + p) for st in streams if st.start <= at + p]
                        read_ready()
                        for st, x in now:
                            while st.done < st.due(x):
                                late = LATE if st in streams else LATE_MAX
                                behind = st.due(x) - st.done
                                near = behind > late and st.need() < pe.time + NEAR or behind > VERY_LATE
                                if not st.step(pe.time) and not (near and st.step()):
                                    break
                                read_ready()
                        while bank is not None and pe.time < bank.time:
                            ahead = [(st.need(), i, st) for i, (st, x) in enumerate(now) if st.done < st.due(x + EARLY)]
                            if not ahead or min(ahead)[0] > bank.time - SLACK or not min(ahead)[2].step():
                                break
                            read_ready()

                    if at == PROJ_START * G and b > 0 and later is not None:
                        later.finish()
                    before, nl = attention_tick(n, qc, kb, before, fill)
                    if nl is not None:
                        if later is not None:
                            later.finish()
                        later = nl
                if n + 1 in maxima:
                    maxima.pop(n + 1).finish()
            for st in streams:
                if b + 1 < nb:
                    st.finish()
        if later is not None:
            later.finish()
        pv(before).finish()
        ending.open = NCH
        ending.finish()
        for r in range(XR):
            for c in range(NCH):
                sp.wait(x_out[r][c].now())

        block = ctx.enter_context(nc.Block())

        @block.tensor
        def _(eng):
            pe.play(eng)

        @block.scalar
        def _(eng):
            act.play(eng)

        @block.vector
        def _(eng):
            dve.play(eng)

        @block.gpsimd
        def _(eng):
            pool.play(eng)

        @block.sync
        def _(eng):
            sp.play(eng)


def rope_tables():
    pos = np.arange(T, dtype=np.float32)[:, None]
    i = np.arange(1, HS // 2 + 1, dtype=np.float32)[None]
    theta = (np.float32(1.0) / np.float32(10000.0) ** (np.float32(2.0) * (i - np.float32(1.0)) / np.float32(HS))).astype(np.float32)
    ang = (pos * theta).astype(np.float32)
    cos, sin = np.cos(ang).T, np.sin(ang).T
    signed = np.stack([-sin, sin])
    cos = np.broadcast_to(cos[None, None, :, None, :], (2, 2, HS // 2, G, T))
    signed = np.broadcast_to(signed[None, :, :, None, :], (2, 2, HS // 2, G, T))
    return (np.ascontiguousarray(cos.reshape(P, T), dtype=np.float32),
            np.ascontiguousarray(signed.reshape(P, T), dtype=np.float32))


def kernel(L0_attn_x, L0_attn_W_qkv, L0_attn_b_qkv, L0_attn_W_proj, L0_attn_b_proj, L0_ffn_W_r, L0_ffn_W_k,
           L0_ffn_W_v, L0_ffn_mu_r, L0_ffn_mu_k):
    import concourse.bacc as bacc
    from concourse.bass_utils import run_bass_kernel_spmd

    x = np.ascontiguousarray(L0_attn_x)
    w = np.asarray(L0_attn_W_qkv).reshape(C, 2, 2, G, 3, HS // 2, 2)
    bq = np.asarray(L0_attn_b_qkv).reshape(2, 2, G, 3, HS // 2, 2)
    w_qk = w[:, :, :, :, 0:2].transpose(0, 4, 1, 2, 6, 5, 3).reshape(C, 2 * C)
    b_qk = bq[:, :, :, 0:2].transpose(3, 0, 1, 5, 4, 2).reshape(4, P).T
    w_v = np.asarray(L0_attn_W_qkv).reshape(C, H, 3, HS)[:, :, 2].reshape(C, C)
    b_v = np.asarray(L0_attn_b_qkv).reshape(H, 3, HS)[:, 2].reshape(1, C)
    rope_c, rope_s = rope_tables()
    arrays = {
        "x": x,
        "w_r": np.asarray(L0_ffn_W_r).T, "w_k": np.asarray(L0_ffn_W_k).T, "w_v": np.asarray(L0_ffn_W_v).T,
        "mu_r": np.asarray(L0_ffn_mu_r).reshape(CC, P).T, "mu_k": np.asarray(L0_ffn_mu_k).reshape(CC, P).T,
        "w_qk": w_qk, "b_qk": b_qk, "w_vv": w_v, "b_v": b_v,
        "w_p": np.asarray(L0_attn_W_proj), "b_p": np.asarray(L0_attn_b_proj).reshape(1, C),
        "rope_c": rope_c, "rope_s": rope_s,
    }
    arrays = {n: np.ascontiguousarray(a) for n, a in arrays.items()}
    nc = bacc.Bacc("TRN2", target_bir_lowering=False, num_devices=1)
    aps = {n: nc.dram_tensor(n, a.shape, mybir.dt.from_np(a.dtype), kind="ExternalInput").ap() for n, a in arrays.items()}
    out = nc.dram_tensor("out", x.shape, mybir.dt.from_np(x.dtype), kind="ExternalOutput").ap()
    macaron(nc, out=out, nb=x.shape[0], **aps)
    r = run_bass_kernel_spmd(nc, [arrays], core_ids=[0])
    return r.results[0]["out"]
```
